# Optimizing a Trainium2 kernel written in Bass

```python
import numpy as np
import jax
import jax.numpy as jnp

def _softmax(x, axis=-1):
    return jax.nn.softmax(x, axis=axis)

def _gelu(x):
    return jax.nn.gelu(x, approximate=True)

def _silu(x):
    return jax.nn.silu(x)

def _sigmoid(x):
    return jax.nn.sigmoid(x)

def _layernorm(x, axis=-1, eps=1e-05):
    m = jnp.mean(x, axis=axis, keepdims=True)
    v = jnp.var(x, axis=axis, keepdims=True)
    return (x - m) / jnp.sqrt(v + eps)

def _scatter_add(tgt, idx, src, axis=0):
    return tgt.at[idx].add(src)

def _segment_sum(src, seg, n):
    return jax.ops.segment_sum(src, seg, n)
kernel_name = 'mk_seq_postln_d2_jaxref_r4_539059'

def setup_inputs(seed: int=0):
    np.random.seed(seed)
    _w = jnp.asarray

    def _L0_attn_setup():
        import jax, jax.numpy as jnp
        import numpy as np
        D_MODEL = 256
        D_STATE = 16
        D_CONV = 4
        EXPAND = 2
        D_INNER = EXPAND * D_MODEL
        DT_RANK = D_MODEL // 16
        BATCH, SEQLEN = (2, 256)

        def _mamba_fwd(hidden_states, in_proj_w, conv1d_w, conv1d_b, x_proj_w, dt_proj_w, dt_proj_b, A_log, D_param, out_proj_w):
            Bsz, L, _ = hidden_states.shape
            xz = jnp.einsum('bld,ed->ble', hidden_states, in_proj_w)
            x, z = jnp.split(xz, 2, axis=-1)
            xc = jnp.transpose(x, (0, 2, 1))
            kern = conv1d_w[:, None, :]
            conv = jax.lax.conv_general_dilated(xc, kern, window_strides=(1,), padding=[(D_CONV - 1, 0)], dimension_numbers=('NCH', 'OIH', 'NCH'), feature_group_count=D_INNER)
            u = jax.nn.silu(conv + conv1d_b[None, :, None])
            ut = jnp.transpose(u, (0, 2, 1))
            x_dbl = jnp.einsum('bld,rd->blr', ut, x_proj_w)
            dt_low = x_dbl[..., :DT_RANK]
            B_var = x_dbl[..., DT_RANK:DT_RANK + D_STATE]
            C_var = x_dbl[..., DT_RANK + D_STATE:]
            delta = jax.nn.softplus(jnp.einsum('blr,dr->bld', dt_low, dt_proj_w) + dt_proj_b)
            A = -jnp.exp(A_log)
            dA = jnp.exp(delta[..., None] * A)
            dBu = delta[..., None] * B_var[:, :, None, :] * ut[..., None]

            def step(h, inp):
                da, dbu, c = inp
                h = da * h + dbu
                y = jnp.einsum('bdn,bn->bd', h, c)
                return (h, y)
            h0 = jnp.zeros((Bsz, D_INNER, D_STATE), dtype=hidden_states.dtype)
            _, ys = jax.lax.scan(step, h0, (jnp.moveaxis(dA, 1, 0), jnp.moveaxis(dBu, 1, 0), jnp.moveaxis(C_var, 1, 0)))
            y = jnp.moveaxis(ys, 0, 1)
            y = y + ut * D_param
            out_z = y * jax.nn.silu(z)
            return jnp.einsum('bld,ed->ble', out_z, out_proj_w)
        key = jax.random.key(seed)
        ks = jax.random.split(key, 9)
        f32 = jnp.float32
        hidden_states = jax.random.normal(ks[0], (BATCH, SEQLEN, D_MODEL), dtype=f32)
        in_proj_w = jax.random.normal(ks[1], (2 * D_INNER, D_MODEL), dtype=f32) * D_MODEL ** (-0.5)
        conv1d_w = jax.random.normal(ks[2], (D_INNER, D_CONV), dtype=f32) * D_CONV ** (-0.5)
        conv1d_b = jax.random.normal(ks[3], (D_INNER,), dtype=f32) * 0.1
        x_proj_w = jax.random.normal(ks[4], (DT_RANK + 2 * D_STATE, D_INNER), dtype=f32) * D_INNER ** (-0.5)
        dt_std = DT_RANK ** (-0.5)
        dt_proj_w = jax.random.uniform(ks[5], (D_INNER, DT_RANK), dtype=f32, minval=-dt_std, maxval=dt_std)
        dt_proj_b = jax.random.normal(ks[6], (D_INNER,), dtype=f32) * 0.1
        A_log = jnp.log(jnp.tile(jnp.arange(1, D_STATE + 1, dtype=f32), (D_INNER, 1)))
        D_param = jnp.ones((D_INNER,), dtype=f32)
        out_proj_w = jax.random.normal(ks[7], (D_MODEL, D_INNER), dtype=f32) * D_INNER ** (-0.5)
        return dict(hidden_states=hidden_states, in_proj_w=in_proj_w, conv1d_w=conv1d_w, conv1d_b=conv1d_b, x_proj_w=x_proj_w, dt_proj_w=dt_proj_w, dt_proj_b=dt_proj_b, A_log=A_log, D_param=D_param, out_proj_w=out_proj_w)
    _L0_attn_in = _L0_attn_setup()

    def _L0_ffn_setup():
        import jax, jax.numpy as jnp
        import numpy as np
        D_MODEL = 256
        D_HIDDEN = 1024
        NUM_EXPERTS = 8
        B, T = (2, 512)
        key = jax.random.key(seed)
        ks = jax.random.split(key, 8)
        s = 0.02
        x = jax.random.normal(ks[0], (B, T, D_MODEL), dtype=jnp.float32)
        Wg = jax.random.normal(ks[1], (D_MODEL, NUM_EXPERTS), dtype=jnp.float32) * s
        bg = jnp.zeros((NUM_EXPERTS,), dtype=jnp.float32)
        W1 = jax.random.normal(ks[2], (NUM_EXPERTS, D_MODEL, D_HIDDEN), dtype=jnp.float32) * s
        b1 = jnp.zeros((NUM_EXPERTS, D_HIDDEN), dtype=jnp.float32)
        W2 = jax.random.normal(ks[3], (NUM_EXPERTS, D_HIDDEN, D_MODEL), dtype=jnp.float32) * s
        b2 = jnp.zeros((NUM_EXPERTS, D_MODEL), dtype=jnp.float32)
        return {'x': x, 'Wg': Wg, 'bg': bg, 'W1': W1, 'b1': b1, 'W2': W2, 'b2': b2}
    _L0_ffn_in = _L0_ffn_setup()

    def _L1_attn_setup():
        import jax, jax.numpy as jnp
        import numpy as np
        D_MODEL = 256
        D_STATE = 16
        D_CONV = 4
        EXPAND = 2
        D_INNER = D_MODEL * EXPAND
        B = 1
        L = 512
        key = jax.random.key(seed)
        ks = jax.random.split(key, 8)
        s = lambda k, shape, scale: jax.random.normal(k, shape, dtype=jnp.float32) * scale
        return {'x': jax.random.normal(ks[0], (B, L, D_MODEL), dtype=jnp.float32), 'in_proj_w': s(ks[1], (D_INNER * 2, D_MODEL), D_MODEL ** (-0.5)), 'conv_w': s(ks[2], (D_INNER, 1, D_CONV), D_CONV ** (-0.5)), 'conv_b': jnp.zeros((D_INNER,), jnp.float32), 'x_proj_w': s(ks[3], (2 * D_STATE + 1, D_INNER), D_INNER ** (-0.5)), 'dt_proj_w': s(ks[4], (D_INNER, 1), 1.0), 'dt_proj_b': jnp.zeros((D_INNER,), jnp.float32), 'A_log': jnp.log(jnp.broadcast_to(jnp.arange(1, D_STATE + 1, dtype=jnp.float32), (D_INNER, D_STATE))), 'D': jnp.ones((D_INNER,), jnp.float32), 'out_proj_w': s(ks[5], (D_MODEL, D_INNER), D_INNER ** (-0.5))}
    _L1_attn_in = _L1_attn_setup()

    def _L1_ffn_setup():
        import jax, jax.numpy as jnp
        import numpy as np
        D_MODEL = 256
        EXPANSION = 4
        D_HIDDEN = D_MODEL * EXPANSION
        NUM_STAGES = int(np.log2(D_HIDDEN))

        def butterfly(y, weights, dim):
            lead = y.shape[:-1]
            for stage in range(weights.shape[0]):
                s = 2 ** stage
                nb = dim // (2 * s)
                yr = y.reshape(*lead, nb, 2, s)
                a = yr[..., 0, :]
                b = yr[..., 1, :]
                w = weights[stage].reshape(nb, s, 2, 2)
                na = w[..., 0, 0] * a + w[..., 0, 1] * b
                nb2 = w[..., 1, 0] * a + w[..., 1, 1] * b
                y = jnp.stack([na, nb2], axis=-2).reshape(*lead, dim)
            return y
        key = jax.random.key(seed)
        ks = jax.random.split(key, 6)
        B, S = (4, 512)
        x = jax.random.normal(ks[0], (B, S, D_MODEL), jnp.float32)
        W_exp = jax.random.normal(ks[1], (D_MODEL, D_HIDDEN), jnp.float32) * 0.02
        b_exp = jnp.zeros((D_HIDDEN,), jnp.float32)
        up_weights = jax.random.normal(ks[2], (NUM_STAGES, D_HIDDEN // 2, 2, 2), jnp.float32) * 0.02
        up_bias = jnp.zeros((D_HIDDEN,), jnp.float32)
        down_weights = jax.random.normal(ks[3], (NUM_STAGES, D_HIDDEN // 2, 2, 2), jnp.float32) * 0.02
        W_con = jax.random.normal(ks[4], (D_HIDDEN, D_MODEL), jnp.float32) * 0.02
        b_con = jnp.zeros((D_MODEL,), jnp.float32)
        down_bias = jnp.zeros((D_MODEL,), jnp.float32)
        return dict(x=x, W_exp=W_exp, b_exp=b_exp, up_weights=up_weights, up_bias=up_bias, down_weights=down_weights, W_con=W_con, b_con=b_con, down_bias=down_bias)
    _L1_ffn_in = _L1_ffn_setup()
    _d = {'L0_attn_hidden_states': _L0_attn_in['hidden_states'], 'L0_attn_in_proj_w': _L0_attn_in['in_proj_w'], 'L0_attn_conv1d_w': _L0_attn_in['conv1d_w'], 'L0_attn_conv1d_b': _L0_attn_in['conv1d_b'], 'L0_attn_x_proj_w': _L0_attn_in['x_proj_w'], 'L0_attn_dt_proj_w': _L0_attn_in['dt_proj_w'], 'L0_attn_dt_proj_b': _L0_attn_in['dt_proj_b'], 'L0_attn_A_log': _L0_attn_in['A_log'], 'L0_attn_D_param': _L0_attn_in['D_param'], 'L0_attn_out_proj_w': _L0_attn_in['out_proj_w'], 'L0_ffn_Wg': _L0_ffn_in['Wg'], 'L0_ffn_bg': _L0_ffn_in['bg'], 'L0_ffn_W1': _L0_ffn_in['W1'], 'L0_ffn_b1': _L0_ffn_in['b1'], 'L0_ffn_W2': _L0_ffn_in['W2'], 'L0_ffn_b2': _L0_ffn_in['b2'], 'L1_attn_in_proj_w': _L1_attn_in['in_proj_w'], 'L1_attn_conv_w': _L1_attn_in['conv_w'], 'L1_attn_conv_b': _L1_attn_in['conv_b'], 'L1_attn_x_proj_w': _L1_attn_in['x_proj_w'], 'L1_attn_dt_proj_w': _L1_attn_in['dt_proj_w'], 'L1_attn_dt_proj_b': _L1_attn_in['dt_proj_b'], 'L1_attn_A_log': _L1_attn_in['A_log'], 'L1_attn_D': _L1_attn_in['D'], 'L1_attn_out_proj_w': _L1_attn_in['out_proj_w'], 'L1_ffn_W_exp': _L1_ffn_in['W_exp'], 'L1_ffn_b_exp': _L1_ffn_in['b_exp'], 'L1_ffn_up_weights': _L1_ffn_in['up_weights'], 'L1_ffn_up_bias': _L1_ffn_in['up_bias'], 'L1_ffn_down_weights': _L1_ffn_in['down_weights'], 'L1_ffn_W_con': _L1_ffn_in['W_con'], 'L1_ffn_b_con': _L1_ffn_in['b_con'], 'L1_ffn_down_bias': _L1_ffn_in['down_bias']}
    _x0 = _d['L0_attn_hidden_states']
    _d['L0_attn_hidden_states'] = jax.random.normal(jax.random.fold_in(jax.random.key(seed), 1), (8, 512, 256), dtype=_x0.dtype)
    del _x0
    return _d

def reference(L0_attn_hidden_states, L0_attn_in_proj_w, L0_attn_conv1d_w, L0_attn_conv1d_b, L0_attn_x_proj_w, L0_attn_dt_proj_w, L0_attn_dt_proj_b, L0_attn_A_log, L0_attn_D_param, L0_attn_out_proj_w, L0_ffn_Wg, L0_ffn_bg, L0_ffn_W1, L0_ffn_b1, L0_ffn_W2, L0_ffn_b2, L1_attn_in_proj_w, L1_attn_conv_w, L1_attn_conv_b, L1_attn_x_proj_w, L1_attn_dt_proj_w, L1_attn_dt_proj_b, L1_attn_A_log, L1_attn_D, L1_attn_out_proj_w, L1_ffn_W_exp, L1_ffn_b_exp, L1_ffn_up_weights, L1_ffn_up_bias, L1_ffn_down_weights, L1_ffn_W_con, L1_ffn_b_con, L1_ffn_down_bias):

    def _L0_attn_ref(hidden_states, in_proj_w, conv1d_w, conv1d_b, x_proj_w, dt_proj_w, dt_proj_b, A_log, D_param, out_proj_w):
        import jax, jax.numpy as jnp
        import numpy as np
        D_MODEL = 256
        D_STATE = 16
        D_CONV = 4
        EXPAND = 2
        D_INNER = EXPAND * D_MODEL
        DT_RANK = D_MODEL // 16
        BATCH, SEQLEN = (2, 256)

        def _mamba_fwd(hidden_states, in_proj_w, conv1d_w, conv1d_b, x_proj_w, dt_proj_w, dt_proj_b, A_log, D_param, out_proj_w):
            Bsz, L, _ = hidden_states.shape
            xz = jnp.einsum('bld,ed->ble', hidden_states, in_proj_w)
            x, z = jnp.split(xz, 2, axis=-1)
            xc = jnp.transpose(x, (0, 2, 1))
            kern = conv1d_w[:, None, :]
            conv = jax.lax.conv_general_dilated(xc, kern, window_strides=(1,), padding=[(D_CONV - 1, 0)], dimension_numbers=('NCH', 'OIH', 'NCH'), feature_group_count=D_INNER)
            u = jax.nn.silu(conv + conv1d_b[None, :, None])
            ut = jnp.transpose(u, (0, 2, 1))
            x_dbl = jnp.einsum('bld,rd->blr', ut, x_proj_w)
            dt_low = x_dbl[..., :DT_RANK]
            B_var = x_dbl[..., DT_RANK:DT_RANK + D_STATE]
            C_var = x_dbl[..., DT_RANK + D_STATE:]
            delta = jax.nn.softplus(jnp.einsum('blr,dr->bld', dt_low, dt_proj_w) + dt_proj_b)
            A = -jnp.exp(A_log)
            dA = jnp.exp(delta[..., None] * A)
            dBu = delta[..., None] * B_var[:, :, None, :] * ut[..., None]

            def step(h, inp):
                da, dbu, c = inp
                h = da * h + dbu
                y = jnp.einsum('bdn,bn->bd', h, c)
                return (h, y)
            h0 = jnp.zeros((Bsz, D_INNER, D_STATE), dtype=hidden_states.dtype)
            _, ys = jax.lax.scan(step, h0, (jnp.moveaxis(dA, 1, 0), jnp.moveaxis(dBu, 1, 0), jnp.moveaxis(C_var, 1, 0)))
            y = jnp.moveaxis(ys, 0, 1)
            y = y + ut * D_param
            out_z = y * jax.nn.silu(z)
            return jnp.einsum('bld,ed->ble', out_z, out_proj_w)
        return _mamba_fwd(hidden_states, in_proj_w, conv1d_w, conv1d_b, x_proj_w, dt_proj_w, dt_proj_b, A_log, D_param, out_proj_w)

    def _L0_ffn_ref(x, Wg, bg, W1, b1, W2, b2):
        import jax, jax.numpy as jnp
        import numpy as np
        D_MODEL = 256
        D_HIDDEN = 1024
        NUM_EXPERTS = 8
        B, T = (2, 512)
        gate_logits = jnp.einsum('btd,de->bte', x, Wg) + bg
        gate_scores = jax.nn.softmax(gate_logits, axis=-1)
        top1_idx = jnp.argmax(gate_scores, axis=-1)
        top1_mask = jax.nn.one_hot(top1_idx, NUM_EXPERTS, dtype=x.dtype)
        top1_weight = jnp.sum(gate_scores * top1_mask, axis=-1, keepdims=True)
        h = jax.nn.silu(jnp.einsum('btd,edh->bteh', x, W1) + b1)
        o = jnp.einsum('bteh,ehd->bted', h, W2) + b2
        y = jnp.sum(o * top1_mask[..., None], axis=2) * top1_weight
        return y

    def _L1_attn_ref(x, in_proj_w, conv_w, conv_b, x_proj_w, dt_proj_w, dt_proj_b, A_log, D, out_proj_w):
        import jax, jax.numpy as jnp
        import numpy as np
        D_MODEL = 256
        D_STATE = 16
        D_CONV = 4
        EXPAND = 2
        D_INNER = D_MODEL * EXPAND
        B = 1
        L = 512
        Bb = x.shape[0]
        xz = x @ in_proj_w.T
        x_ssm, z = jnp.split(xz, 2, axis=-1)
        xt = jnp.swapaxes(x_ssm, 1, 2)
        xc = jax.lax.conv_general_dilated(xt, conv_w, window_strides=(1,), padding=[(D_CONV - 1, 0)], feature_group_count=D_INNER, dimension_numbers=('NCH', 'OIH', 'NCH'))
        xc = xc + conv_b[None, :, None]
        xc = jax.nn.silu(jnp.swapaxes(xc, 1, 2))
        A = -jnp.exp(A_log)
        xp = xc @ x_proj_w.T
        dt_r = xp[..., :1]
        Bv = xp[..., 1:1 + D_STATE]
        Cv = xp[..., 1 + D_STATE:]
        dt = jax.nn.softplus(dt_r @ dt_proj_w.T + dt_proj_b)
        dA = jnp.exp(dt[..., None] * A)
        dBx = dt[..., None] * Bv[:, :, None, :] * xc[..., None]

        def step(h, inps):
            dA_t, dBx_t, C_t = inps
            h = dA_t * h + dBx_t
            y = jnp.einsum('bdn,bn->bd', h, C_t)
            return (h, y)
        h0 = jnp.zeros((Bb, D_INNER, D_STATE), x.dtype)
        _, ys = jax.lax.scan(step, h0, (jnp.swapaxes(dA, 0, 1), jnp.swapaxes(dBx, 0, 1), jnp.swapaxes(Cv, 0, 1)))
        y = jnp.swapaxes(ys, 0, 1) + xc * D
        return y * jax.nn.silu(z) @ out_proj_w.T

    def _L1_ffn_ref(x, W_exp, b_exp, up_weights, up_bias, down_weights, W_con, b_con, down_bias):
        import jax, jax.numpy as jnp
        import numpy as np
        D_MODEL = 256
        EXPANSION = 4
        D_HIDDEN = D_MODEL * EXPANSION
        NUM_STAGES = int(np.log2(D_HIDDEN))

        def butterfly(y, weights, dim):
            lead = y.shape[:-1]
            for stage in range(weights.shape[0]):
                s = 2 ** stage
                nb = dim // (2 * s)
                yr = y.reshape(*lead, nb, 2, s)
                a = yr[..., 0, :]
                b = yr[..., 1, :]
                w = weights[stage].reshape(nb, s, 2, 2)
                na = w[..., 0, 0] * a + w[..., 0, 1] * b
                nb2 = w[..., 1, 0] * a + w[..., 1, 1] * b
                y = jnp.stack([na, nb2], axis=-2).reshape(*lead, dim)
            return y
        h = jnp.einsum('bsd,dh->bsh', x, W_exp) + b_exp
        h = butterfly(h, up_weights, D_HIDDEN)
        h = jax.nn.gelu(h + up_bias, approximate=False)
        h = butterfly(h, down_weights, D_HIDDEN)
        y = jnp.einsum('bsh,hd->bsd', h, W_con) + b_con
        return y + down_bias
    x = L0_attn_hidden_states
    x = _layernorm(x + _L0_attn_ref(x, L0_attn_in_proj_w, L0_attn_conv1d_w, L0_attn_conv1d_b, L0_attn_x_proj_w, L0_attn_dt_proj_w, L0_attn_dt_proj_b, L0_attn_A_log, L0_attn_D_param, L0_attn_out_proj_w), axis=-1)
    x = _layernorm(x + _L0_ffn_ref(x, L0_ffn_Wg, L0_ffn_bg, L0_ffn_W1, L0_ffn_b1, L0_ffn_W2, L0_ffn_b2), axis=-1)
    x = _layernorm(x + _L1_attn_ref(x, L1_attn_in_proj_w, L1_attn_conv_w, L1_attn_conv_b, L1_attn_x_proj_w, L1_attn_dt_proj_w, L1_attn_dt_proj_b, L1_attn_A_log, L1_attn_D, L1_attn_out_proj_w), axis=-1)
    x = _layernorm(x + _L1_ffn_ref(x, L1_ffn_W_exp, L1_ffn_b_exp, L1_ffn_up_weights, L1_ffn_up_bias, L1_ffn_down_weights, L1_ffn_W_con, L1_ffn_b_con, L1_ffn_down_bias), axis=-1)
    return x

_drawn_inputs = setup_inputs


def setup_inputs(seed=0):
    import zlib

    import numpy as np

    out = dict(_drawn_inputs(seed))
    spreads = {'L0_attn_D_param': (1.0, 0.2),
     'L0_ffn_bg': (0.0, 0.439),
     'L0_ffn_b1': (0.0, 0.8),
     'L0_ffn_b2': (0.0, 0.321),
     'L1_attn_conv_b': (0.0, 0.1),
     'L1_attn_dt_proj_b': (0.0, 0.321),
     'L1_attn_D': (1.0, 0.2),
     'L1_ffn_b_exp': (0.0, 0.1),
     'L1_ffn_up_bias': (0.0, 0.1),
     'L1_ffn_b_con': (0.0, 0.1),
     'L1_ffn_down_bias': (0.0, 0.1)}
    factors = {}
    for name, (base, spread) in spreads.items():
        noise = np.random.default_rng([zlib.crc32(name.encode()), seed]).standard_normal(out[name].shape)
        drawn = base * np.exp(spread * noise) if base else spread * noise
        out[name] = jnp.asarray(drawn.astype(out[name].dtype))
    for name, factor in factors.items():
        out[name] = (out[name] * factor).astype(out[name].dtype)
    return out
```

```python
import concourse.bass as bass
from concourse import mybir
from contextlib import ExitStack

FP32 = mybir.dt.float32
ALU = mybir.AluOpType
ACT = mybir.ActivationFunctionType
AX = mybir.AxisListType


def ge(engine, semaphore, value):
    if not isinstance(value, int) or value > 0:
        engine.wait_ge(semaphore, value)


def build(nc, hbm, out):
    P = 128
    B, L, D = hbm["L0_x"].shape
    DI, DCONV = hbm["L0_conv_w"].shape
    N = hbm["L0_A_log"].shape[1]
    C = DI // P
    K = D // P
    TT = L // P
    NT = B * TT
    RANKS = [hbm["L0_dt_w"].shape[0], hbm["L1_dt_w"].shape[0]]
    RMAX = max(RANKS)
    E, _, F = hbm["W1"].shape
    FB = F // P
    TS = 2 * P
    TR = TS // P
    SMAX = B * L // TS
    TILES = (B * L - E) // TS + E
    STAGES = hbm["up_w"].shape[0]
    NEAR = P.bit_length() - 1
    FAR = STAGES - NEAR
    EPS = 1e-5
    PAD = DCONV - 1

    ctx = ExitStack()
    with ctx:
        def sb(name, shape, dt=FP32):
            return ctx.enter_context(nc.sbuf_tensor(name, shape, dt))

        def sem(name):
            return ctx.enter_context(nc.semaphore(name))

        x = sb("x", [P, NT, D])
        ident = sb("ident", [P, P])
        w_in = sb("w_in", [P, K, 2 * DI])
        w_out = sb("w_out", [P, C, D])
        w_x = sb("w_x", [P, C, RMAX + 2 * N])
        w_dt = sb("w_dt", [2 * N + RMAX, DI])
        conv_w = sb("conv_w", [P, C, DCONV])
        a_log = sb("a_log", [P, C, N])
        a_neg = sb("a_neg", [P, C, N])
        chan = sb("chan", [P, 3, C])
        stats = sb("stats", [P, TT, 6])
        mv = sb("mv", [P, TT, 2])
        ve = sb("ve", [P, TT])
        rstd = sb("rstd", [P, TT])
        neg_half = sb("neg_half", [P, TT])
        zero_row = sb("zero_row", [P, 1, D])
        up_b = sb("up_b", [P, FB])
        gelu_b = sb("gelu_b", [P, FB])

        BCS, HS, AS = 4, 4, 4
        with ExitStack() as own:
            def sb1(name, shape, dt=FP32):
                return own.enter_context(nc.sbuf_tensor(name, shape, dt))
            xs = sb1("xs", [P, TT, D])
            xT = sb1("xT", [P, 2, K, L])
            xpad = sb1("xpad", [P, C, L + PAD])
            u = sb1("u", [P, 2, C, L])
            yz = sb1("yz", [P, C, L])
            delta = sb1("delta", [P, 2, C, L])
            du = sb1("du", [P, C, L])
            xd_row = sb1("xd_row", [2 * N + RMAX, L])
            b_row = sb1("b_row", [P, BCS, L])
            c_row = sb1("c_row", [P, BCS, L])
            hst = sb1("hst", [P, HS, C, L])
            dA = sb1("dA", [P, AS, C, L])
            prod = sb1("prod", [P, 2, C, L])

        U32, I32 = mybir.dt.uint32, mybir.dt.int32
        with ExitStack() as own:
            def sb2(name, shape, dt=FP32):
                return own.enter_context(nc.sbuf_tensor(name, shape, dt))
            gate_w = sb2("gate_w", [P, K, E])
            gate_b = sb2("gate_b", [P, 1, E])
            g_rows = sb2("g_rows", [P, 2, TT, D])
            g_cols = sb2("g_cols", [P, 2, K, L])
            before_m = sb2("before_m", [P, P])
            ones = sb2("ones", [P, P])
            prio = sb2("prio", [P, 1, E])
            steps = sb2("steps", [P, 1, SMAX])
            tile_no = sb2("tile_no", [P, TILES, 1])
            restart = sb2("restart", [P, E, NT])
            lg = sb2("lg", [P, NT, E])
            eq = sb2("eq", [P, NT, E])
            pick = sb2("pick", [P, NT, E])
            top = sb2("top", [P, NT])
            w_top = sb2("w_top", [P, NT])
            tot = sb2("tot", [P, E, NT])
            cum = sb2("cum", [P, E, NT])
            cmp_s = sb2("cmp_s", [P, E, SMAX])
            n_tiles = sb2("n_tiles", [P, E])
            end_tile = sb2("end_tile", [P, E])
            first_tile = sb2("first_tile", [P, E])
            cmp_t = sb2("cmp_t", [P, TILES, E])
            tile_e = sb2("tile_e", [P, TILES])
            tile_i = sb2("tile_i", [P, TILES], I32)
            dest_f = sb2("dest_f", [P, NT])
            dest = sb2("dest", [P, NT], U32)
            w1 = sb2("w1", [P, 2, K, F])
            w2 = sb2("w2", [P, 2, FB, D])
            b1 = sb2("b1", [P, 2, FB])
            b2 = sb2("b2", [P, 2, D])
            xg = sb2("xg", [P, 2, TR, D])
            xgT = sb2("xgT", [P, K, TS])
            hid = sb2("hid", [P, FB, TS])
            yt = sb2("yt", [P, 2, TR, D])
            with ExitStack() as prep:
                def sb3(name, shape, dt=FP32):
                    return prep.enter_context(nc.sbuf_tensor(name, shape, dt))
                DA = D + 1
                bf_w = sb3("bf_w", [P, 2, 4 * F // 2])
                bf_m = sb3("bf_m", [P, 2, F])
                bf_t = sb3("bf_t", [P, 2, F])
                far_w = sb3("far_w", [P, 2, FAR, FB // 2, 4])
                va = sb3("va", [P, FB, DA])
                vb = sb3("vb", [P, FB, DA])
                far_t = sb3("far_t", [P, 2, FB // 2, DA])
                m_T = sb3("m_T", [P, FB, P])
            yg = sb2("yg", [P, NT, D])

        with ExitStack() as own:
            def sb4(name, shape, dt=FP32):
                return own.enter_context(nc.sbuf_tensor(name, shape, dt))
            f_up = sb4("f_up", [P, K, F])
            f_down = sb4("f_down", [P, FB, D])
            f_bias = sb4("f_bias", [P, 2, D])
            f_rows = sb4("f_rows", [P, 2, TT, D])
            f_cols = sb4("f_cols", [P, K, L])
            f_hid = sb4("f_hid", [P, FB, L])

        yb = [ctx.enter_context(nc.psum_tensor(f"y{c}", [P, L], FP32)) for c in range(C)]
        pj = [ctx.enter_context(nc.psum_tensor(f"pj{i}", [P, L], FP32)) for i in range(4)]

        banks = yb + pj
        w_exp_v = w1[:, :, :, :].rearrange("p s k f -> p (s k f)")[:, 0:FB * DA].rearrange("p (f d) -> p f d", d=DA)
        up_v = w2[:, :, :, :].rearrange("p s f d -> p (s f d)")[:, 0:FB * DA].rearrange("p (f d) -> p f d", d=DA)
        up_w = w_exp_v

        x_sorted = nc.dram_tensor("x_sorted", [TILES * TS, D], FP32, kind="Internal").ap()
        y_sorted = nc.dram_tensor("y_sorted", [TILES * TS, D], FP32, kind="Internal").ap()
        up_dense = nc.dram_tensor("up_dense", [P, K * F], FP32, kind="Internal").ap()
        down_dense = nc.dram_tensor("down_dense", [P, FB * D], FP32, kind="Internal").ap()
        xdbl = nc.dram_tensor("xdbl_scratch", [2, 2 * N * L], FP32, kind="Internal").ap()

        x0_loaded, x_loaded, w_loaded = sem("x0_loaded"), sem("x_loaded"), sem("w_loaded")
        const_made, ident_made, pads_zeroed = sem("const_made"), sem("ident_made"), sem("pads_zeroed")
        a_exp, a_ready = sem("a_exp"), sem("a_ready")
        xs_loaded = sem("xs_loaded")
        xT_ps, xT_sb = sem("xT_ps"), sem("xT_sb")
        xin_ps, xin_sb = sem("xin_ps"), sem("xin_sb")
        conv_tap, u_ready = sem("conv_tap"), sem("u_ready")
        xdbl_ps, xdbl_sb, bc_stored = sem("xdbl_ps"), sem("xdbl_sb"), sem("bc_stored")
        b_loaded = [sem(f"b_loaded{i}") for i in range(BCS)]
        c_loaded = [sem(f"c_loaded{i}") for i in range(BCS)]
        dt_ps, dt_sb, sp_exp, ln_ready = sem("dt_ps"), sem("dt_sb"), sem("sp_exp"), sem("ln_ready")
        delta_ready, du_ready = sem("delta_ready"), sem("du_ready")
        z_ps, z_sb, zs_ready = sem("z_ps"), sem("z_sb"), sem("zs_ready")
        dA_ready, dbu_made, scan_done = sem("dA_ready"), sem("dbu_made"), sem("scan_done")
        prod_made, y_summed, y_free = sem("prod_made"), sem("y_summed"), sem("y_free")
        yz_ready, out_ps, res_done = sem("yz_ready"), sem("out_ps"), sem("res_done")
        stat_done, aggr_done, var_ready = sem("stat_done"), sem("aggr_done"), sem("var_ready")
        rstd_ready, norm_done = sem("rstd_ready"), sem("norm_done")
        out_stored = sem("out_stored")
        waits_passed = sem("waits_passed")
        zero_made, sorted_zeroed = sem("zero_made"), sem("sorted_zeroed")
        gate_loaded, moe_const = sem("gate_loaded"), sem("moe_const")
        g_loaded = [sem("g_loaded0"), sem("g_loaded1")]
        g_rows_free, g_cols_free = sem("g_rows_free"), sem("g_cols_free")
        gT_ps, gT_sb = sem("gT_ps"), sem("gT_sb")
        route, gate_exp, picked, ranked, routed = (sem("route"), sem("gate_exp"), sem("picked"), sem("ranked"),
                                                   sem("routed"))
        scattered, gathered, gathered_added = sem("scattered"), sem("gathered"), sem("gathered_added")
        tile_loaded = [sem("tile_loaded0"), sem("tile_loaded1")]
        y_stored = [sem("y_stored0"), sem("y_stored1")]
        tile_free, yt_made = sem("tile_free"), sem("yt_made")
        tT_ps, tT_sb, hid_ps, hid_sb, yt_ps = (sem("tT_ps"), sem("tT_sb"), sem("hid_ps"), sem("hid_sb"),
                                               sem("yt_ps"))
        bf_loaded = [sem("bf_loaded0"), sem("bf_loaded1")]
        bf_step, far_loaded, dense_loaded = sem("bf_step"), sem("far_loaded"), sem("dense_loaded")
        far_step, up_ps, up_sb, down_ps, down_sb = (sem("far_step"), sem("up_ps"), sem("up_sb"), sem("down_ps"),
                                                    sem("down_sb"))
        upT_ps, upT_sb, mT_ps, mT_sb, folded = sem("upT_ps"), sem("upT_sb"), sem("mT_ps"), sem("mT_sb"), sem("folded")
        far_part = sem("far_part")
        dense_stored, up_folded, down_folded = sem("dense_stored"), sem("up_folded"), sem("down_folded")
        f_loaded, f_rows_loaded = sem("f_loaded"), [sem("f_rows_loaded0"), sem("f_rows_loaded1")]
        f_rows_free, fT_ps, fT_sb = sem("f_rows_free"), sem("fT_ps"), sem("fT_sb")
        fh_ps, fh_sb, fy_ps, fy_free, f_added = (sem("fh_ps"), sem("fh_sb"), sem("fy_ps"), sem("fy_free"),
                                                 sem("f_added"))

        def half(t, b):
            flat = t[:, :, :, :].rearrange("p h c l -> p (h c l)")
            return flat[:, bass.ds((b % 2) * (C * L), C * L)]

        def chunk(t, b, c, skip=0):
            flat = t[:, :, :, :].rearrange("p h c l -> p (h c l)")
            return flat[:, bass.ds((b % 2) * (C * L) + c * L + skip, L - skip)]

        def columns(p, k):
            return xT[:, :, :, :].rearrange("p h k l -> p (h k l)")[:, bass.ds((p % 2) * (K * L) + k * L, L)]

        def over_batches(engine, before, body):
            before()
            body(0)
            with engine.Fori(1, B - 1) as b:
                body(b)
            body(B - 1)

        def is_first(b):
            return isinstance(b, int) and b == 0

        def is_last(b):
            return isinstance(b, int) and b == B - 1

        W_DMAS = 9

        SP_AT = dict(xs=6)
        AHEAD = 3
        PE_AT = dict(T=0, X=(1, 1, 2, 3), xdbl=6, dt=9, out=(2, 4, 5, 8), Z=(9, 10, 11, 12))
        ACT_AT = dict(xT=3, xin=(5, 5, 7, 7), u=8, xdbl=11, dt=13, sp=14, z=(14, 15, 15, 15))
        DVE_AT = dict(conv=(4, 5), deltas=13, res=(7, 10), stats=10, apply=15, gate=1)

        block = ctx.enter_context(nc.Block())

        def ge_alone(engine, semaphore, value):
            if not isinstance(value, int) or value > 0:
                engine.wait_ge(semaphore, value)
                if not isinstance(value, int):
                    engine.sem_inc(waits_passed, 1)

        @block.sync
        def _(sp):
            def load_weights(lay):
                p = f"L{lay}_"
                R = RANKS[lay]
                for dst, src in (
                    (w_in[:, :, :], hbm[p + "w_in"].rearrange("(k p) e -> p k e", p=P)),
                    (w_x[:, :, 0:R + 2 * N], hbm[p + "w_x"].rearrange("(c p) r -> p c r", p=P)),
                    (w_dt[2 * N:2 * N + R, :], hbm[p + "dt_w"]),
                    (conv_w[:, :, :], hbm[p + "conv_w"].rearrange("(c p) k -> p c k", p=P)),
                    (a_log[:, :, :], hbm[p + "A_log"].rearrange("(c p) n -> p c n", p=P)),
                    (chan[:, 0, :], hbm[p + "conv_b"]),
                    (chan[:, 1, :], hbm[p + "dt_b"]),
                    (chan[:, 2, :], hbm[p + "D"]),
                    (w_out[:, :, :], hbm[p + "w_out"].rearrange("(c p) d -> p c d", p=P)),
                ):
                    sp.dma_start(dst, src).then_inc(w_loaded, 16)

            def load_xs(p):
                sp.dma_start(xs[:, :, :].rearrange("p i d -> p (i d)"),
                             x[:, bass.ds(p * TT, TT), :].rearrange("p i d -> p (i d)")).then_inc(xs_loaded, 16)

            def load_state_rows(lay):
                load_xs(0)
                sp.wait_ge(xT_ps, K * (lay * B + 1))
                if lay == 0:
                    sp.wait_ge(x_loaded, 16)
                load_xs(1)
                sp.wait_ge(bc_stored, 16 * (lay * B + 1))
                for n in range(AHEAD):
                    load_b(lay * B, n)
                batch(0, lay * B, True, True)
                with sp.Fori(1, B - 2) as b:
                    batch(b, b + lay * B, True, True)
                batch(B - 2, B - 2 + lay * B, False, True)
                batch(B - 1, B - 1 + lay * B, False, False)

            def row(g, i, ring, n):
                src = xdbl[bass.ds(g % 2, 1), bass.ds(i * L, L)]
                return sp.dma_start(ring[:, n % BCS, :], src.broadcast_to([P, L]))

            def load_b(g, n):
                ge(sp, dbu_made, N * g + n - BCS + 1)
                row(g, 2 * n, b_row, n).then_inc(b_loaded[n % BCS], 16)

            def load_c(g, n):
                ge(sp, prod_made, N * g + n - BCS + 1)
                row(g, 2 * n + 1, c_row, n).then_inc(c_loaded[n % BCS], 16)

            def batch(b, g, load_rows, has_next):
                for n in range(N):
                    if load_rows and n == SP_AT["xs"]:
                        sp.wait_ge(xT_ps, K * (g + 2))
                        load_xs(b + 2)
                    if n + AHEAD < N:
                        load_b(g, n + AHEAD)
                    elif has_next:
                        if n + AHEAD == N:
                            sp.wait_ge(bc_stored, 16 * (g + 2))
                        load_b(g + 1, n + AHEAD - N)
                    load_c(g, n)

            def batch_rows(p):
                return x[:, bass.ds(p * TT, TT), :].rearrange("p i d -> p (i d)")

            def load_gate_rows():
                with sp.Fori(0, B // 2) as h:
                    for s in range(2):
                        sp.wait_ge(g_rows_free, 2 * h + s + 1)
                        sp.dma_start(g_rows[:, s, :, :].rearrange("p i d -> p (i d)"),
                                     batch_rows(2 * h + s)).then_inc(g_loaded[s], 16)

            def load_tile(j, s, first):
                sp.wait_ge(tile_free, j + 1)
                sp.wait_ge(yt_made, j + 1)
                e = sp.value_load(tile_i[0:1, bass.ds(j, 1)], min_val=0, max_val=E - 1)
                for dst, src in (
                    (w1[:, s, :, :], hbm["W1"][bass.ds(e, 1), :, :].rearrange("o (k p) f -> p (o k) f", p=P)),
                    (b1[:, s, :], hbm["b1"][bass.ds(e, 1), :, :].rearrange("o p f -> p (o f)")),
                    (w2[:, s, :, :], hbm["W2"][bass.ds(e, 1), :, :].rearrange("o (f p) d -> p (o f) d", p=P)),
                    (b2[:, s, :], hbm["b2"][bass.ds(e, 1), :].broadcast_to([P, D])),
                ):
                    sp.dma_start(dst, src).then_inc(tile_loaded[s], 16)
                if first:
                    sp.wait_ge(scattered, 16 * NT)
                sp.dma_start(xg[:, s, :, :], x_sorted[bass.ds(j * TS, TS), :].rearrange("(r p) d -> p r d", p=P)
                             ).then_inc(tile_loaded[s], 16)

            def store_tile(j, s):
                sp.wait_ge(yt_made, j + 3)
                sp.dma_start(y_sorted[bass.ds(j * TS, TS), :].rearrange("(r p) d -> p r d", p=P),
                             yt[:, s, :, :]).then_inc(y_stored[s], 16)

            def experts():
                sp.wait_ge(norm_done, B)
                for dst, src in (
                    (gate_w[:, :, :], hbm["gate_w"].rearrange("(k p) e -> p k e", p=P)),
                    (gate_b[:, 0, :], hbm["gate_b"].broadcast_to([P, E])),
                ):
                    sp.dma_start(dst, src).then_inc(gate_loaded, 16)
                load_gate_rows()
                for dst, src in (
                    (far_w[:, 0, :, :, :], hbm["up_w"][NEAR:STAGES, :, :].rearrange("s (q p) w -> p s q w", p=P)),
                    (far_w[:, 1, :, :, :], hbm["down_w"][NEAR:STAGES, :, :].rearrange("s (q p) w -> p s q w", p=P)),
                    (va[:, :, 0:D], hbm["w_con"].rearrange("(f p) d -> p f d", p=P)),
                    (up_b[:, :], hbm["up_bias"]),
                ):
                    sp.dma_start(dst, src).then_inc(far_loaded, 16)
                load_weights(1)
                sp.wait_ge(routed, 1)
                load_tile(0, 0, True)
                load_tile(1, 1, False)
                with sp.Fori(1, TILES // 2) as h:
                    for s in range(2):
                        load_tile(2 * h + s, s, False)
                        store_tile(2 * h + s - 2, s)
                load_tile(TILES - 1, 0, False)
                for j in (TILES - 3, TILES - 2, TILES - 1):
                    store_tile(j, j % 2)
                sp.wait_ge(tile_free, TILES + 2)
                sp.dma_start(w_exp_v, hbm["w_exp"].rearrange("(f p) d -> p f d", p=P)).then_inc(dense_loaded, 16)
                sp.wait_ge(down_folded, 1)
                sp.dma_start(down_dense, bf_m[:, :, :].rearrange("p a f -> p (a f)")).then_inc(dense_stored, 16)
                sp.wait_ge(up_folded, 1)
                sp.dma_start(up_dense, bf_t[:, :, :].rearrange("p a f -> p (a f)")).then_inc(dense_stored, 16)

            def last_layer():
                sp.wait_ge(norm_done, 3 * B)
                sp.wait_ge(dense_stored, 32)
                for dst, src in (
                    (f_up[:, :, :].rearrange("p k f -> p (k f)"), up_dense),
                    (f_down[:, :, :].rearrange("p f d -> p (f d)"), down_dense),
                    (f_bias[:, 0, :], hbm["b_con"].broadcast_to([P, D])),
                    (f_bias[:, 1, :], hbm["down_bias"].broadcast_to([P, D])),
                ):
                    sp.dma_start(dst, src).then_inc(f_loaded, 16)
                with sp.Fori(0, B // 2) as h:
                    for s in range(2):
                        sp.wait_ge(f_rows_free, 2 * h + s + 1)
                        sp.dma_start(f_rows[:, s, :, :].rearrange("p i d -> p (i d)"),
                                     batch_rows(2 * h + s)).then_inc(f_rows_loaded[s], 16)

            rows = hbm["L0_x"].rearrange("b (i p) d -> p (b i) d", p=P)
            sp.dma_start(x[:, 0:TT, :], rows[:, 0:TT, :]).then_inc(x0_loaded, 16)
            load_weights(0)
            sp.dma_start(x[:, TT:NT, :], rows[:, TT:NT, :]).then_inc(x_loaded, 16)
            sp.wait_ge(zero_made, 1)
            sp.dma_start(x_sorted.rearrange("(n p) d -> p n d", p=P),
                         zero_row[:, :, :].broadcast_to([P, TILES * TR, D])).then_inc(sorted_zeroed, 16)
            sp.wait_ge(x0_loaded, 16)
            load_state_rows(0)
            experts()
            sp.wait_ge(norm_done, 2 * B)
            sp.wait_ge(dense_stored, 32)
            load_state_rows(1)
            last_layer()

        @block.gpsimd
        def _(pool):
            nc.gpsimd.memset(neg_half[:, :], -0.5).then_inc(const_made, 1)
            nc.gpsimd.memset(ident[:, :], 0.0).then_inc(const_made, 1)
            nc.gpsimd.memset(zero_row[:, :, :], 0.0).then_inc(zero_made, 1)
            pool.wait_ge(const_made, 2)
            nc.gpsimd.affine_select(out=ident[:, :], in_=ident[:, :], compare_op=ALU.not_equal, fill=1.0,
                                    base=0, pattern=[[-1, P]], channel_multiplier=1).then_inc(ident_made, 1)

            def norm_power(q):
                pool.wait_ge(var_ready, q + 1)
                nc.gpsimd.tensor_tensor(out=rstd[:, :], in0=ve[:, :], in1=neg_half[:, :],
                                        op=ALU.pow).then_inc(rstd_ready, 1)

            def mamba(lay):
                def body(b):
                    g = b + lay * B
                    for n in range(N):
                        if n == 0:
                            ge_alone(pool, delta_ready, g + 1)
                            ge_alone(pool, u_ready, g + 1)
                            ge_alone(pool, dbu_made, N * g)
                            nc.gpsimd.tensor_tensor(out=du[:, :, :].rearrange("p c l -> p (c l)"), in0=half(delta, b),
                                                    in1=half(u, b), op=ALU.mult).then_inc(du_ready, 1)
                            ge_alone(pool, du_ready, g + 1)
                        ge_alone(pool, b_loaded[n % BCS], 16 * (N // BCS * g + n // BCS + 1))
                        ge_alone(pool, prod_made, N * g + n - HS + 1)
                        nc.gpsimd.tensor_tensor(
                            out=hst[:, n % HS, :, :],
                            in0=du[:, :, :],
                            in1=b_row[:, n % BCS:n % BCS + 1, :].broadcast_to([P, C, L]),
                            op=ALU.mult).then_inc(dbu_made, 1)
                    if not is_first(b):
                        norm_power(g - 1 + lay * B)

                over_batches(pool, lambda: None, body)
                norm_power(2 * lay * B + B - 1)

            def experts():
                pool.wait_ge(norm_done, B)
                nc.gpsimd.memset(before_m[:, :], 1.0).then_inc(moe_const, 1)
                nc.gpsimd.memset(ones[:, :], 1.0).then_inc(moe_const, 1)
                nc.gpsimd.memset(restart[:, :, :], 1.0).then_inc(moe_const, 1)
                pool.wait_ge(moe_const, 3)
                nc.gpsimd.affine_select(out=before_m[:, :], in_=before_m[:, :], compare_op=ALU.is_gt, fill=0.0,
                                        base=0, pattern=[[1, P]], channel_multiplier=-1).then_inc(moe_const, 1)
                nc.gpsimd.memset(restart[:, :, 0:1], 0.0).then_inc(moe_const, 1)
                for t, pattern, base in ((prio, [[-1, E]], E), (steps, [[TS, SMAX]], 0), (tile_no, [[1, TILES]], 0)):
                    nc.gpsimd.iota(t[:, :, :].rearrange("p a b -> p (a b)"), pattern=pattern, base=base,
                                   channel_multiplier=0,
                                   allow_small_or_imprecise_dtypes=True).then_inc(moe_const, 1)
                pool.wait_ge(sorted_zeroed, 16)
                pool.wait_ge(routed, 1)
                for t in range(NT):
                    nc.gpsimd.indirect_dma_start(
                        out=x_sorted, out_offset=bass.IndirectOffsetOnAxis(ap=dest[:, t:t + 1], axis=0),
                        in_=x[:, t, :], in_offset=None).then_inc(scattered, 16)
                near_butterflies()
                pool.wait_ge(dense_stored, 32)
                for s in range(2):
                    pool.wait_ge(y_stored[s], 16 * ((TILES + 1 - s) // 2))
                for t in range(NT):
                    nc.gpsimd.indirect_dma_start(
                        out=yg[:, t, :], out_offset=None,
                        in_=y_sorted, in_offset=bass.IndirectOffsetOnAxis(ap=dest[:, t:t + 1], axis=0)
                        ).then_inc(gathered, 16)
                with pool.Fori(B, 2 * B) as q:
                    norm_power(q)

            def near_butterflies():
                done = 0
                for half_, name in enumerate(("up_w", "down_w")):
                    for b in range(FB):
                        nc.gpsimd.tensor_copy(bf_m[:, half_, b * P:(b + 1) * P], ident[:, :]).then_inc(bf_step, 1)
                    done += FB
                    for stage in range(NEAR):
                        i = half_ * NEAR + stage
                        st = 1 << stage
                        if stage == 0:
                            load_near(name, 0, i)
                        pool.wait_ge(bf_step, done)
                        if stage + 1 < NEAR:
                            load_near(name, stage + 1, i + 1)
                        pool.wait_ge(bf_loaded[i % 2], 16 * (i // 2 + 1))
                        m = bf_m[:, half_, :].rearrange("p (n two s) -> p n two s", two=2, s=st)
                        w = bf_w[:, i % 2, :].rearrange("p (n s r c) -> p n r s c", s=st, r=2, c=2)
                        o = [bf_t[:, t, :].rearrange("p (n r s) -> p n r s", r=2, s=st) for t in range(2)]
                        shape = [P, F // (2 * st), 2, st]
                        for col in range(2):
                            nc.gpsimd.tensor_tensor(out=o[col], in0=w[:, :, :, :, col],
                                                    in1=m[:, :, col:col + 1, :].broadcast_to(shape),
                                                    op=ALU.mult).then_inc(bf_step, 1)
                        done += 2
                        pool.wait_ge(bf_step, done)
                        nc.gpsimd.tensor_tensor(out=bf_m[:, half_, :], in0=bf_t[:, 0, :], in1=bf_t[:, 1, :],
                                                op=ALU.add).then_inc(bf_step, 1)
                        done += 1
                pool.wait_ge(bf_step, done)
                pool.sem_inc(folded, 1)

            def load_near(name, stage, i):
                w = hbm[name][stage:stage + 1, :, :].rearrange("s k w -> s (k w)")
                pool.dma_start(bf_w[:, i % 2, :], w.broadcast_to([P, 4 * F // 2])).then_inc(bf_loaded[i % 2], 16)

            def last_layer():
                def store(p):
                    norm_power(3 * B + p)
                    ge_alone(pool, norm_done, 3 * B + p + 1)
                    pool.dma_start(out.rearrange("b (i p) d -> p (b i) d", p=P)[:, bass.ds(p * TT, TT), :],
                                   x[:, bass.ds(p * TT, TT), :]).then_inc(out_stored, 16)
                with pool.Fori(0, B) as p:
                    store(p)
                pool.wait_ge(out_stored, 16 * B)

            mamba(0)
            experts()
            mamba(1)
            last_layer()

        @block.scalar
        def _(act):
            def pre_xT(p, g):
                for k in range(K):
                    ge_alone(act, xT_ps, K * g + k + 1)
                    if k == 0:
                        ge_alone(act, z_ps, C * (g - 1))
                    nc.scalar.activation(columns(p, k), pj[k][:, :], ACT.Copy).then_inc(xT_sb, 1)

            def pre_xin(p, g, c):
                ge_alone(act, xin_ps, C * g + c + 1)
                if c == 0:
                    ge_alone(act, delta_ready, g)
                    ge_alone(act, yz_ready, g - 1)
                bank = pj[(c + 2) % 4]
                nc.scalar.activation(xpad[:, c, PAD:PAD + L], bank[:, :], ACT.Copy)
                nc.scalar.activation(chunk(u, p, c), bank[:, :], ACT.Identity,
                                     scale=conv_w[:, c, PAD:PAD + 1]).then_inc(xin_sb, 1)

            def pre_u(p, g):
                ge_alone(act, conv_tap, C * PAD * (g + 1))
                for c in range(C):
                    i = nc.scalar.activation(chunk(u, p, c), chunk(u, p, c), ACT.Silu, bias=chan[:, 0, c:c + 1])
                i.then_inc(u_ready, 1)

            def pre_xdbl(p, g, R):
                ge_alone(act, xdbl_ps, g + 1)
                ge_alone(act, bc_stored, 16 * g)
                ge_alone(act, dt_ps, C * g)
                nc.scalar.activation(xd_row[0:2 * N + R, :], pj[0][0:2 * N + R, :], ACT.Copy).then_inc(xdbl_sb, 1)
                ge_alone(act, xdbl_sb, g + 1)
                ge_alone(act, dbu_made, N * (g - 1))
                ge_alone(act, prod_made, N * (g - 1))
                act.dma_start(xdbl[bass.ds(p % 2, 1), :].rearrange("o (r l) -> (o r) l", l=L),
                              xd_row[0:2 * N, :]).then_inc(bc_stored, 16)

            def pre_dt(p, g):
                for c in range(C):
                    ge_alone(act, dt_ps, C * g + c + 1)
                    if c == 0:
                        ge_alone(act, du_ready, g - 1)
                        ge_alone(act, dA_ready, N * (g - 1))
                    nc.scalar.activation(xpad[:, c, PAD:PAD + L], pj[c % 2][:, :], ACT.Abs,
                                         bias=chan[:, 1, c:c + 1])
                    nc.scalar.activation(chunk(delta, p, c), pj[c % 2][:, :], ACT.Relu,
                                         bias=chan[:, 1, c:c + 1]).then_inc(dt_sb, 1)

            def pre_softplus(p, g):
                ge_alone(act, dt_sb, C * g + C)
                nc.scalar.activation(xpad[:, :, PAD:PAD + L], xpad[:, :, PAD:PAD + L], ACT.Exp,
                                     scale=-1.0).then_inc(sp_exp, 1)
                ge_alone(act, sp_exp, g + 1)
                nc.scalar.activation(xpad[:, :, PAD:PAD + L], xpad[:, :, PAD:PAD + L], ACT.Ln,
                                     bias=1.0).then_inc(ln_ready, 1)

            def gate_z(g, lo, hi):
                for c in range(lo, hi):
                    ge_alone(act, z_ps, C * g + c + 1)
                    if c == 0:
                        ge_alone(act, out_ps, 2 * g)
                    nc.scalar.activation(yz[:, c, :], pj[2 + c % 2][:, :], ACT.Copy).then_inc(z_sb, 1)
                if hi == C:
                    ge_alone(act, z_sb, C * (g + 1))
                    nc.scalar.activation(yz[:, :, :], yz[:, :, :], ACT.Silu).then_inc(zs_ready, 1)

            def mamba(lay):
                R = RANKS[lay]

                def before():
                    act.wait_ge(w_loaded, 16 * W_DMAS * (lay + 1))
                    ge_alone(act, a_ready, lay)
                    nc.scalar.activation(a_neg[:, :, :], a_log[:, :, :], ACT.Exp).then_inc(a_exp, 1)
                    g = lay * B
                    act.wait_ge(pads_zeroed, lay + 1)
                    pre_xT(0, g)
                    for c in range(C):
                        pre_xin(0, g, c)
                    pre_u(0, g)
                    pre_xdbl(0, g, R)
                    pre_dt(0, g)
                    pre_softplus(0, g)
                    act.wait_ge(a_ready, lay + 1)

                def body(b):
                    g = b + lay * B
                    for n in range(N):
                        if n == 0:
                            ge_alone(act, delta_ready, g + 1)
                        ge_alone(act, scan_done, N * g + n - AS + 1)
                        for c in range(C):
                            i = nc.scalar.activation(dA[:, n % AS, c, 1:L], chunk(delta, b, c, 1), ACT.Exp,
                                                     scale=a_neg[:, c, n:n + 1])
                        i.then_inc(dA_ready, 1)
                        if not is_last(b):
                            if n == ACT_AT["xT"]:
                                pre_xT(b + 1, g + 1)
                            for c in range(C):
                                if n == ACT_AT["xin"][c]:
                                    pre_xin(b + 1, g + 1, c)
                            if n == ACT_AT["u"]:
                                pre_u(b + 1, g + 1)
                            if n == ACT_AT["xdbl"]:
                                pre_xdbl(b + 1, g + 1, R)
                            if n == ACT_AT["dt"]:
                                pre_dt(b + 1, g + 1)
                            if n == ACT_AT["sp"]:
                                pre_softplus(b + 1, g + 1)
                        for c in range(C):
                            if n == ACT_AT["z"][c]:
                                gate_z(g, c, c + 1)

                over_batches(act, before, body)

            def experts():
                with act.Fori(0, B // 2) as h:
                    for s in range(2):
                        p = 2 * h + s
                        act.wait_ge(g_cols_free, p + 1)
                        for k in range(K):
                            act.wait_ge(gT_ps, K * p + k + 1)
                            nc.scalar.activation(g_cols[:, s, k, :], banks[2 * s + k][:, :], ACT.Copy
                                                 ).then_inc(gT_sb, 1)
                act.wait_ge(route, 3)
                nc.scalar.activation(eq[:, :, :], eq[:, :, :], ACT.Exp).then_inc(gate_exp, 1)

                def tile(j, s):
                    act.wait_ge(tT_ps, j + 1)
                    nc.scalar.activation(xgT[:, :, :].rearrange("p k t -> p (k t)"), banks[s][:, :], ACT.Copy
                                         ).then_inc(tT_sb, 1)
                    for q in range(FB // 2):
                        act.wait_ge(hid_ps, FB // 2 * j + q + 1)
                        for f in (2 * q, 2 * q + 1):
                            i = nc.scalar.activation(hid[:, f, :], banks[2 + q][:, (f % 2) * TS:(f % 2 + 1) * TS],
                                                     ACT.Silu, bias=b1[:, s, f:f + 1])
                        i.then_inc(hid_sb, 1)

                with act.Fori(0, TILES // 2) as h:
                    for s in range(2):
                        tile(2 * h + s, s)
                tile(TILES - 1, 0)
                for b in range(FB):
                    act.wait_ge(mT_ps, b + 1)
                    nc.scalar.activation(m_T[:, b, :], banks[b][:, 0:P], ACT.Copy).then_inc(mT_sb, 1)
                for b in range(FB):
                    act.wait_ge(up_ps, b + 1)
                    if b == 0:
                        act.wait_ge(far_step, 9)
                    nc.scalar.activation(va[:, b, :], banks[b][:, 0:DA], ACT.Copy).then_inc(up_sb, 1)
                dst = bf_m[:, :, :].rearrange("p a (f d) -> p (a f) d", d=D)
                for b in range(FB):
                    act.wait_ge(down_ps, b + 1)
                    i = nc.scalar.activation(dst[:, b, :], banks[b][:, 0:D], ACT.Copy)
                    i.then_inc(down_sb, 1)
                act.wait_ge(down_sb, FB)
                act.sem_inc(down_folded, 1)
                for b in range(FB):
                    act.wait_ge(upT_ps, b + 1)
                    i = nc.scalar.activation(bf_t[:, :, b * P:(b + 1) * P],
                                             banks[b][:, 0:2 * P].rearrange("p (k f) -> p k f", k=K), ACT.Copy)
                    i.then_inc(upT_sb, 1)
                act.wait_ge(upT_sb, FB)
                act.sem_inc(up_folded, 1)

            def last_layer():
                act.wait_ge(f_loaded, 64)
                with act.Fori(0, B) as p:
                    for k in range(K):
                        act.wait_ge(fT_ps, K * p + k + 1)
                        nc.scalar.activation(f_cols[:, k, :], banks[k][:, :], ACT.Copy).then_inc(fT_sb, 1)
                    for f in range(FB):
                        act.wait_ge(fh_ps, FB * p + f + 1)
                        nc.scalar.activation(f_hid[:, f, :], banks[2 + f % 4][:, :], ACT.Gelu,
                                             bias=gelu_b[:, f:f + 1]).then_inc(fh_sb, 1)

            mamba(0)
            experts()
            mamba(1)
            last_layer()

        @block.tensor
        def _(pe):
            pe.wait_ge(ident_made, 1)

            def pre_T(p, g):
                ge(pe, xs_loaded, 16 * (g + 1))
                for k in range(K):
                    ge(pe, dt_sb, C * g - 1 + k)
                    for i in range(TT):
                        t = nc.tensor.transpose(pj[k][:, i * P:(i + 1) * P],
                                                xs[:, i, k * P:(k + 1) * P], ident[:, :])
                    t.then_inc(xT_ps, 1)

            def pre_X(p, g, c):
                if c == 0:
                    ge(pe, xT_sb, K * (g + 1))
                if c < 2:
                    ge(pe, z_sb, C * (g - 1) - 1 + c)
                for k in range(K):
                    i = nc.tensor.matmul(pj[(c + 2) % 4][:, :], w_in[:, k, c * P:(c + 1) * P], columns(p, k),
                                         start=(k == 0), stop=(k == K - 1))
                i.then_inc(xin_ps, 1)

            def pre_xdbl(p, g, R):
                ge(pe, u_ready, g + 1)
                for c in range(C):
                    i = nc.tensor.matmul(pj[0][0:2 * N + R, :], w_x[:, c, 0:2 * N + R], chunk(u, p, c),
                                         start=(c == 0), stop=(c == C - 1))
                i.then_inc(xdbl_ps, 1)

            def pre_dt(p, g, R):
                ge(pe, xdbl_sb, g + 1)
                low = slice(2 * N, 2 * N + R)
                for c in range(C):
                    if c >= 2:
                        ge(pe, dt_sb, C * g + c - 1)
                    nc.tensor.matmul(pj[c % 2][:, :], w_dt[low, c * P:(c + 1) * P], xd_row[low, :],
                                     start=True, stop=True).then_inc(dt_ps, 1)

            def gate_Z(p, g, c):
                if c < 2:
                    ge(pe, res_done, 2 * g - 1 + c)
                else:
                    ge(pe, z_sb, C * g + c - 1)
                for k in range(K):
                    i = nc.tensor.matmul(pj[2 + c % 2][:, :], w_in[:, k, DI + c * P:DI + (c + 1) * P],
                                         columns(p, k),
                                         start=(k == 0), stop=(k == K - 1))
                i.then_inc(z_ps, 1)

            def project(g, i, interleaved):
                if i == 0:
                    ge(pe, yz_ready, g + 1)
                if i % 2 == 0:
                    if interleaved:
                        ge(pe, xin_sb, C * (g + 2) + 1 + i // 2)
                    else:
                        ge(pe, z_sb, C * (g + 1))
                bank = pj[2 + i // 2][:, (i % 2) * D:(i % 2 + 1) * D]
                for c in range(C):
                    lhsT = yz[:, c, i * P:(i + 1) * P]
                    m = nc.tensor.matmul(bank, lhsT, w_out[:, c, :], start=(c == 0), stop=(c == C - 1))
                if i % 2 == 1:
                    m.then_inc(out_ps, 1)

            def mamba(lay):
                R = RANKS[lay]

                def before():
                    g = lay * B
                    pe.wait_ge(w_loaded, 16 * W_DMAS * (lay + 1))
                    if lay == 0:
                        pe.wait_ge(x0_loaded, 16)
                    pre_T(0, g)
                    for c in range(C):
                        pre_X(0, g, c)
                    pre_xdbl(0, g, R)
                    pre_dt(0, g, R)

                def body(b):
                    g = b + lay * B
                    for n in range(N):
                        ge(pe, prod_made, N * g + n + 1)
                        for c in range(C):
                            if n == 0:
                                ge(pe, y_free, C * (g - 1) + c + 1)
                            i = nc.tensor.matmul(yb[c][:, :], ident[:, :], prod[:, n % 2, c, :],
                                                 start=(n == 0), stop=(n == N - 1))
                        i.then_inc(y_summed, 1)
                        if not is_last(b):
                            if n == PE_AT["T"]:
                                pre_T(b + 1, g + 1)
                            for c in range(C):
                                if n == PE_AT["X"][c]:
                                    pre_X(b + 1, g + 1, c)
                            if n == PE_AT["xdbl"]:
                                pre_xdbl(b + 1, g + 1, R)
                            if n == PE_AT["dt"]:
                                pre_dt(b + 1, g + 1, R)
                        for i in range(TT):
                            if not is_first(b) and n == PE_AT["out"][i]:
                                project(g - 1, i, not is_last(b))
                        for c in range(C):
                            if n == PE_AT["Z"][c]:
                                gate_Z(b, g, c)

                over_batches(pe, before, body)
                for i in range(TT):
                    project(lay * B + B - 1, i, False)

            def experts():
                pe.wait_ge(norm_done, B)
                pe.sem_inc(g_rows_free, 2)
                pe.sem_inc(g_cols_free, 2)
                pe.sem_inc(tile_free, 2)
                pe.wait_ge(gate_loaded, 32)
                with pe.Fori(0, B // 2) as h:
                    for s in range(2):
                        p = 2 * h + s
                        pe.wait_ge(g_loaded[s], 16 * (h + 1))
                        for k in range(K):
                            for i in range(TT):
                                t = nc.tensor.transpose(banks[2 * s + k][:, i * P:(i + 1) * P],
                                                        g_rows[:, s, i, k * P:(k + 1) * P], ident[:, :])
                            t.then_inc(gT_ps, 1)
                        pe.wait_ge(gT_sb, K * (p + 1))
                        pe.sem_inc(g_rows_free, 1)
                        for i in range(TT):
                            for k in range(K):
                                m = nc.tensor.matmul(pj[0][:, bass.ds((p * TT + i) * E, E)],
                                                     g_cols[:, s, k, i * P:(i + 1) * P], gate_w[:, k, :],
                                                     start=(k == 0), stop=(k == K - 1))
                        m.then_inc(g_cols_free, 1)
                pe.wait_ge(moe_const, 8)
                pe.wait_ge(picked, 1)
                flat = pick[:, :, :].rearrange("p t e -> p (t e)")
                nc.tensor.matmul(pj[1][:, 0:NT * E], before_m[:, :], flat, start=True, stop=True)
                nc.tensor.matmul(pj[2][:, 0:NT * E], ones[:, :], flat, start=True, stop=True).then_inc(ranked, 1)

                def tile(j, s, h):
                    pe.wait_ge(tile_loaded[s], 16 * 5 * (h + 1))
                    for k in range(K):
                        for r in range(TR):
                            t = nc.tensor.transpose(banks[s][:, k * TS + r * P:k * TS + (r + 1) * P],
                                                    xg[:, s, r, k * P:(k + 1) * P], ident[:, :])
                    t.then_inc(tT_ps, 1)
                    pe.wait_ge(tT_sb, j + 1)
                    for f in range(FB):
                        for k in range(K):
                            m = nc.tensor.matmul(banks[2 + f // 2][:, (f % 2) * TS:(f % 2 + 1) * TS],
                                                 w1[:, s, k, f * P:(f + 1) * P], xgT[:, k, :],
                                                 start=(k == 0), stop=(k == K - 1))
                        if f % 2:
                            m.then_inc(hid_ps, 1)
                    pe.wait_ge(yt_made, j + 1)
                    for r in range(TR):
                        for f in range(FB):
                            if r == 0 and f % 2 == 0:
                                pe.wait_ge(hid_sb, FB // 2 * j + f // 2 + 1)
                            m = nc.tensor.matmul(banks[6 + s][:, r * D:(r + 1) * D],
                                                 hid[:, f, r * P:(r + 1) * P], w2[:, s, f, :],
                                                 start=(f == 0), stop=(f == FB - 1))
                    m.then_inc(yt_ps, 1)
                    pe.wait_ge(yt_ps, j + 1)
                    pe.sem_inc(tile_free, 1)

                with pe.Fori(0, TILES // 2) as h:
                    for s in range(2):
                        tile(2 * h + s, s, h)
                tile(TILES - 1, 0, TILES // 2)

                pe.wait_ge(folded, 1)
                pe.wait_ge(yt_made, TILES + 2)
                for b in range(FB):
                    nc.tensor.transpose(banks[b][:, 0:P], bf_m[:, 1, b * P:(b + 1) * P], ident[:, :]).then_inc(mT_ps, 1)
                pe.wait_ge(dense_loaded, 16)
                for b in range(FB):
                    pe.wait_ge(mT_sb, b + 1)
                    nc.tensor.matmul(banks[b][:, 0:DA], bf_m[:, 0, b * P:(b + 1) * P], w_exp_v[:, b, :],
                                     start=True, stop=True).then_inc(up_ps, 1)
                pe.wait_ge(far_step, 9)
                for b in range(FB):
                    pe.wait_ge(up_sb, b + 1)
                    nc.tensor.matmul(banks[b][:, 0:D], m_T[:, b, :], vb[:, b, 0:D],
                                     start=True, stop=True).then_inc(down_ps, 1)
                pe.wait_ge(far_step, 18)
                for b in range(FB):
                    pe.wait_ge(down_sb, b + 1)
                    for k in range(K):
                        t = nc.tensor.transpose(banks[b][:, k * P:(k + 1) * P], up_v[:, b, k * P:(k + 1) * P],
                                                ident[:, :])
                    t.then_inc(upT_ps, 1)

            def last_layer():
                pe.wait_ge(norm_done, 3 * B)
                pe.sem_inc(f_rows_free, 2)
                pe.sem_inc(fy_free, 2)
                pe.wait_ge(f_loaded, 64)
                with pe.Fori(0, B // 2) as h:
                    for s in range(2):
                        p = 2 * h + s
                        pe.wait_ge(f_rows_loaded[s], 16 * (h + 1))
                        for k in range(K):
                            for i in range(TT):
                                t = nc.tensor.transpose(banks[k][:, i * P:(i + 1) * P],
                                                        f_rows[:, s, i, k * P:(k + 1) * P], ident[:, :])
                            t.then_inc(fT_ps, 1)
                        pe.wait_ge(fT_sb, K * (p + 1))
                        pe.sem_inc(f_rows_free, 1)
                        for f in range(FB):
                            if f >= 4:
                                pe.wait_ge(fh_sb, FB * p + f - 3)
                            for k in range(K):
                                m = nc.tensor.matmul(banks[2 + f % 4][:, :], f_up[:, k, f * P:(f + 1) * P],
                                                     f_cols[:, k, :], start=(k == 0), stop=(k == K - 1))
                            m.then_inc(fh_ps, 1)
                        for i in range(TT):
                            if i % 2 == 0:
                                pe.wait_ge(fy_free, 2 * p + i // 2 + 1)
                            for f in range(FB):
                                if i == 0:
                                    pe.wait_ge(fh_sb, FB * p + f + 1)
                                m = nc.tensor.matmul(banks[6 + i // 2][:, (i % 2) * D:(i % 2 + 1) * D],
                                                     f_hid[:, f, i * P:(i + 1) * P], f_down[:, f, :],
                                                     start=(f == 0), stop=(f == FB - 1))
                            if i % 2:
                                m.then_inc(fy_ps, 1)

            mamba(0)
            experts()
            mamba(1)
            last_layer()

        @block.vector
        def _(dve):
            def conv(p, g, h):
                ge(dve, xin_sb, C * g + 2 * h + 2)
                for k in range(PAD):
                    if k:
                        ge(dve, conv_tap, C * PAD * g + 2 * PAD * h + 2 * k)
                    for c in (2 * h, 2 * h + 1):
                        nc.vector.scalar_tensor_tensor(
                            out=chunk(u, p, c), in0=xpad[:, c, k:k + L], scalar=conv_w[:, c, k:k + 1],
                            in1=chunk(u, p, c), op0=ALU.mult, op1=ALU.add).then_inc(conv_tap, 1)

            def deltas(p, g):
                ge(dve, ln_ready, g + 1)
                d3 = half(delta, p).rearrange("p (c l) -> p c l", c=C)
                nc.vector.tensor_tensor(out=d3, in0=d3, in1=xpad[:, :, PAD:PAD + L],
                                        op=ALU.add).then_inc(delta_ready, 1)

            def scan(b, g, n):
                ge(dve, dA_ready, N * g + n + 1)
                ge(dve, dbu_made, N * g + n + 1)
                h = hst[:, n % HS, :, :].rearrange("p c l -> p (c l)")
                nc.vector.tensor_tensor_scan(out=h, data0=dA[:, n % AS, :, :].rearrange("p c l -> p (c l)"),
                                             data1=h, initial=0.0, op0=ALU.mult,
                                             op1=ALU.add).then_inc(scan_done, 1)

            def add_skip(e, g):
                ge(dve, y_summed, N * (g + 1))
                for c in range(C):
                    nc.vector.scalar_tensor_tensor(out=chunk(u, e, c), in0=chunk(u, e, c),
                                                   scalar=chan[:, 2, c:c + 1], in1=yb[c][:, :],
                                                   op0=ALU.mult, op1=ALU.add).then_inc(y_free, 1)

            def gate(e, g):
                ge(dve, y_free, C * (g + 1))
                ge(dve, zs_ready, g + 1)
                nc.vector.tensor_tensor(out=yz[:, :, :], in0=half(u, e).rearrange("p (c l) -> p c l", c=C),
                                        in1=yz[:, :, :], op=ALU.mult).then_inc(yz_ready, 1)

            def rows(e, i, n):
                return x[:, bass.ds(e * TT + i, n), :]

            def residual(e, g, j):
                ge(dve, out_ps, 2 * g + j + 1)
                r = rows(e, 2 * j, 2)
                nc.vector.tensor_tensor(out=r, in0=r, in1=pj[2 + j][:, :].rearrange("p (i d) -> p i d", d=D),
                                        op=ALU.add).then_inc(res_done, 1)

            def norm_stats(e, g):
                for i in range(TT):
                    s = nc.vector.bn_stats(out=stats[:, i, :], in_=rows(e, i, 1).rearrange("p o d -> p (o d)"))
                s.then_inc(stat_done, 1)
                ge_alone(dve, stat_done, g + 1)
                for i in range(TT):
                    s = nc.vector.bn_aggr(out=mv[:, i, :], in_=stats[:, i, :])
                s.then_inc(aggr_done, 1)
                ge_alone(dve, aggr_done, g + 1)
                nc.vector.tensor_scalar(ve[:, :], mv[:, :, 1], EPS, None, ALU.add).then_inc(var_ready, 1)

            def norm_apply(e, g):
                ge(dve, rstd_ready, g + 1)
                for i in range(TT):
                    r = rows(e, i, 1).rearrange("p o d -> p (o d)")
                    s = nc.vector.tensor_scalar(r, r, mv[:, i, 0:1], rstd[:, i:i + 1], ALU.subtract, ALU.mult)
                s.then_inc(norm_done, 1)

            def mamba(lay):
                def before():
                    g = lay * B
                    if lay:
                        dve.wait_ge(norm_done, 2 * B)
                        dve.wait_ge(dense_stored, 32)
                    nc.vector.memset(xpad[:, :, 0:PAD], 0.0)
                    nc.vector.memset(dA[:, :, :, 0:1], 0.0).then_inc(pads_zeroed, 1)
                    dve.wait_ge(pads_zeroed, lay + 1)
                    dve.wait_ge(w_loaded, 16 * W_DMAS * (lay + 1))
                    dve.wait_ge(a_exp, lay + 1)
                    nc.vector.tensor_scalar(a_neg[:, :, :], a_neg[:, :, :], -1.0, None, ALU.mult).then_inc(a_ready, 1)
                    conv(0, g, 0)
                    conv(0, g, 1)
                    deltas(0, g)

                def body(b):
                    g = b + lay * B
                    scan(b, g, 0)
                    for n in range(N):
                        if 0 < n < N - 1:
                            scan(b, g, n + 1)
                        ge(dve, scan_done, N * g + n + 1)
                        ge(dve, c_loaded[n % BCS], 16 * (N // BCS * g + n // BCS + 1))
                        ge(dve, y_summed, N * g + n - 1)
                        nc.vector.tensor_tensor(out=prod[:, n % 2, :, :], in0=hst[:, n % HS, :, :],
                                                in1=c_row[:, n % BCS:n % BCS + 1, :].broadcast_to([P, C, L]),
                                                op=ALU.mult).then_inc(prod_made, 1)
                        if n == 0:
                            if not is_first(b):
                                add_skip(b - 1, g - 1)
                            scan(b, g, 1)
                        if not is_first(b) and n == DVE_AT["gate"]:
                            gate(b - 1, g - 1)
                        if not is_last(b):
                            for h in range(2):
                                if n == DVE_AT["conv"][h]:
                                    conv(b + 1, g + 1, h)
                            if n == DVE_AT["deltas"]:
                                deltas(b + 1, g + 1)
                        if not is_first(b):
                            for h in range(2):
                                if n == DVE_AT["res"][h]:
                                    residual(b - 1, g - 1, h)
                            if n == DVE_AT["stats"]:
                                ge_alone(dve, res_done, 2 * g)
                                norm_stats(b - 1, g - 1 + lay * B)
                            if n == DVE_AT["apply"]:
                                norm_apply(b - 1, g - 1 + lay * B)

                over_batches(dve, before, body)
                e, g = B - 1, lay * B + B - 1
                add_skip(e, g)
                gate(e, g)
                residual(e, g, 0)
                residual(e, g, 1)
                dve.wait_ge(res_done, 2 * g + 2)
                norm_stats(e, g + lay * B)
                norm_apply(e, g + lay * B)

            def experts():
                step = [0]

                def link(i):
                    step[0] += 1
                    i.then_inc(route, 1)
                    dve.wait_ge(route, step[0])

                V = nc.vector
                dve.sem_inc(yt_made, 2)
                dve.wait_ge(g_cols_free, B + 2)
                dve.wait_ge(moe_const, 8)
                te = [P, NT, E]
                link(V.tensor_tensor(out=lg[:, :, :], in0=pj[0][:, 0:NT * E].rearrange("p (t e) -> p t e", e=E),
                                     in1=gate_b[:, :, :].broadcast_to(te), op=ALU.add))
                link(V.tensor_reduce(out=top[:, :], in_=lg[:, :, :], axis=AX.X, op=ALU.max))
                topb = top[:, :].rearrange("p (t o) -> p t o", o=1).broadcast_to(te)
                link(V.tensor_tensor(out=eq[:, :, :], in0=lg[:, :, :], in1=topb, op=ALU.subtract))
                link(V.tensor_tensor(out=lg[:, :, :], in0=lg[:, :, :], in1=topb, op=ALU.is_equal))
                link(V.tensor_tensor(out=lg[:, :, :], in0=lg[:, :, :], in1=prio[:, :, :].broadcast_to(te),
                                     op=ALU.mult))
                link(V.tensor_reduce(out=top[:, :], in_=lg[:, :, :], axis=AX.X, op=ALU.max))
                V.tensor_tensor(out=pick[:, :, :], in0=lg[:, :, :], in1=topb, op=ALU.is_equal).then_inc(picked, 1)
                dve.wait_ge(gate_exp, 1)
                link(V.tensor_reduce(out=w_top[:, :], in_=eq[:, :, :], axis=AX.X, op=ALU.add))
                link(V.reciprocal(w_top[:, :], w_top[:, :]))
                dve.wait_ge(ranked, 1)
                et = [P, E, NT]
                link(V.tensor_copy(tot[:, :, :], pj[2][:, 0:NT * E].rearrange("p (t e) -> p e t", e=E)))
                link(V.tensor_tensor_scan(out=cum[:, :, :].rearrange("p e t -> p (e t)"),
                                          data0=restart[:, :, :].rearrange("p e t -> p (e t)"),
                                          data1=tot[:, :, :].rearrange("p e t -> p (e t)"),
                                          initial=0.0, op0=ALU.mult, op1=ALU.add))
                es = [P, E, SMAX]
                link(V.tensor_tensor(out=cmp_s[:, :, :], in0=cum[:, :, NT - 1:NT].broadcast_to(es),
                                     in1=steps[:, :, :].broadcast_to(es), op=ALU.is_gt))
                link(V.tensor_reduce(out=n_tiles[:, :], in_=cmp_s[:, :, :], axis=AX.X, op=ALU.add))
                link(V.tensor_tensor_scan(out=end_tile[:, :], data0=ones[:, 0:E], data1=n_tiles[:, :],
                                          initial=0.0, op0=ALU.mult, op1=ALU.add))
                link(V.tensor_tensor(out=first_tile[:, :], in0=end_tile[:, :], in1=n_tiles[:, :], op=ALU.subtract))
                link(V.tensor_tensor(out=cum[:, :, :], in0=cum[:, :, :], in1=tot[:, :, :], op=ALU.subtract))
                link(V.scalar_tensor_tensor(
                    out=cum[:, :, :], in0=first_tile[:, :].rearrange("p (e o) -> p e o", o=1).broadcast_to(et),
                    scalar=float(TS), in1=cum[:, :, :], op0=ALU.mult, op1=ALU.add))
                link(V.tensor_tensor(out=lg[:, :, :], in0=cum[:, :, :].rearrange("p e t -> p t e"),
                                     in1=pj[1][:, 0:NT * E].rearrange("p (t e) -> p t e", e=E), op=ALU.add))
                link(V.tensor_tensor(out=lg[:, :, :], in0=lg[:, :, :], in1=pick[:, :, :], op=ALU.mult))
                link(V.tensor_reduce(out=dest_f[:, :], in_=lg[:, :, :], axis=AX.X, op=ALU.add))
                link(V.tensor_copy(dest[:, :], dest_f[:, :]))
                ct = [P, TILES, E]
                link(V.tensor_tensor(out=cmp_t[:, :, :],
                                     in0=end_tile[:, :].rearrange("p (o e) -> p o e", o=1).broadcast_to(ct),
                                     in1=tile_no[:, :, :].broadcast_to(ct), op=ALU.is_le))
                link(V.tensor_reduce(out=tile_e[:, :], in_=cmp_t[:, :, :], axis=AX.X, op=ALU.add))
                link(V.tensor_scalar(tile_e[:, :], tile_e[:, :], float(E - 1), None, ALU.min))
                link(V.tensor_copy(tile_i[:, :], tile_e[:, :]))
                dve.sem_inc(routed, 1)

                dve.wait_ge(far_loaded, 64)
                far_stages(va, vb, va, 1, D, 0)

                def tile(j, s, h):
                    dve.wait_ge(yt_ps, j + 1)
                    if not isinstance(h, int) or h > 0:
                        ge_alone(dve, y_stored[s], 16 * h)
                    V.tensor_tensor(out=yt[:, s, :, :],
                                    in0=banks[6 + s][:, :].rearrange("p (r d) -> p r d", d=D),
                                    in1=b2[:, s:s + 1, :].broadcast_to([P, TR, D]), op=ALU.add).then_inc(yt_made, 1)

                tile(0, 0, 0)
                tile(1, 1, 0)
                with dve.Fori(1, TILES // 2) as h:
                    for s in range(2):
                        tile(2 * h + s, s, h)
                tile(TILES - 1, 0, TILES // 2)

                dve.wait_ge(up_sb, FB)
                dve.wait_ge(yt_ps, TILES)
                far_stages(va, up_v, up_w, 0, DA, 9)
                V.tensor_tensor(out=gelu_b[:, :], in0=up_v[:, :, D], in1=up_b[:, :], op=ALU.add)

                dve.wait_ge(gathered, 16 * NT)
                with dve.Fori(0, B) as e:
                    for i in range(TT):
                        t = e * TT + i
                        r = rows(e, i, 1).rearrange("p o d -> p (o d)")
                        a = V.scalar_tensor_tensor(
                            out=r, in0=yg[:, bass.ds(t, 1), :].rearrange("p o d -> p (o d)"),
                            scalar=w_top[:, bass.ds(t, 1)], in1=r, op0=ALU.mult, op1=ALU.add)
                    a.then_inc(gathered_added, 1)
                    ge_alone(dve, gathered_added, e + 1)
                    norm_stats(e, B + e)
                    norm_apply(e, B + e)

            def far_stages(src, dst, mid, half_, width, done):
                order = range(FAR) if half_ == 0 else range(FAR - 1, -1, -1)
                bufs = [src, dst, mid, dst]
                for n, stage in enumerate(order):
                    bl = 1 << stage
                    a_in = bufs[n][:, :, 0:width].rearrange("p (n two b) d -> p n two b d", two=2, b=bl)
                    a_out = bufs[n + 1][:, :, 0:width].rearrange("p (n two b) d -> p n two b d", two=2, b=bl)
                    w = far_w[:, half_, stage, :, :].rearrange("p (n b) w -> p n b w", b=bl)
                    shape = [P, FB // 2 // bl, bl, width]
                    tmp = [far_t[:, t, :, 0:width].rearrange("p (n b) d -> p n b d", b=bl) for t in range(2)]
                    for r in range(2):
                        for c in range(2):
                            wi = 2 * r + c if half_ == 0 else 2 * c + r
                            i = nc.vector.tensor_tensor(out=tmp[c], in0=a_in[:, :, c, :, :],
                                                        in1=w[:, :, :, wi:wi + 1].broadcast_to(shape), op=ALU.mult)
                        i.then_inc(far_part, 1)
                        far_parts[0] += 1
                        dve.wait_ge(far_part, far_parts[0])
                        i = nc.vector.tensor_tensor(out=a_out[:, :, r, :, :], in0=tmp[0], in1=tmp[1], op=ALU.add)
                        i.then_inc(far_part, 1)
                        far_parts[0] += 1
                        dve.wait_ge(far_part, far_parts[0])
                dve.sem_inc(far_step, 9)

            far_parts = [0]

            def last_layer():
                with dve.Fori(0, B) as p:
                    for j in range(2):
                        dve.wait_ge(fy_ps, 2 * p + j + 1)
                        r = rows(p, 2 * j, 2)
                        nc.vector.tensor_tensor(out=r, in0=r,
                                                in1=banks[6 + j][:, :].rearrange("p (i d) -> p i d", d=D),
                                                op=ALU.add).then_inc(fy_free, 1)
                    dve.wait_ge(fy_free, 2 * p + 4)
                    r = rows(p, 0, TT)
                    for half_ in range(2):
                        nc.vector.tensor_tensor(out=r, in0=r,
                                                in1=f_bias[:, half_:half_ + 1, :].broadcast_to([P, TT, D]),
                                                op=ALU.add).then_inc(f_added, 1)
                        ge_alone(dve, f_added, 2 * p + half_ + 1)
                    norm_stats(p, 3 * B + p)
                    norm_apply(p, 3 * B + p)

            mamba(0)
            experts()
            mamba(1)
            last_layer()


def kernel(**inputs):
    import numpy as np
    import concourse.bacc as bacc
    from concourse import mybir as mb
    from concourse.bass_utils import run_bass_kernel_spmd

    nc = bacc.Bacc("TRN2", target_bir_lowering=False, num_devices=1, dynamic_dma_scratch_size=4096)
    A = {k: np.asarray(v) for k, v in inputs.items()}

    def per_channel(v):
        return v.reshape(-1, 128).T

    def state_rows_in_pairs(w, rank):
        n = (w.shape[0] - rank) // 2
        b, c = w[rank:rank + n], w[rank + n:]
        return np.concatenate([np.stack([b, c], 1).reshape(2 * n, -1), w[:rank]], 0).T

    lay = {"L0_x": A["L0_attn_hidden_states"]}
    names = {0: ("conv1d_w", "conv1d_b", "D_param"), 1: ("conv_w", "conv_b", "D")}
    for n in (0, 1):
        q, (cw, cb, dn) = f"L{n}_attn_", names[n]
        lay[f"L{n}_w_in"] = A[q + "in_proj_w"].T
        lay[f"L{n}_conv_w"] = A[q + cw].reshape(-1, A[q + cw].shape[-1])
        lay[f"L{n}_conv_b"] = per_channel(A[q + cb])
        lay[f"L{n}_w_x"] = state_rows_in_pairs(A[q + "x_proj_w"], A[q + "dt_proj_w"].shape[1])
        lay[f"L{n}_dt_w"] = A[q + "dt_proj_w"].T
        lay[f"L{n}_dt_b"] = per_channel(A[q + "dt_proj_b"])
        lay[f"L{n}_A_log"] = A[q + "A_log"]
        lay[f"L{n}_D"] = per_channel(A[q + dn])
        lay[f"L{n}_w_out"] = A[q + "out_proj_w"].T
    f0, f1 = "L0_ffn_", "L1_ffn_"
    lay["gate_w"], lay["gate_b"] = A[f0 + "Wg"], A[f0 + "bg"].reshape(1, -1)
    lay["W1"], lay["W2"], lay["b2"] = A[f0 + "W1"], A[f0 + "W2"], A[f0 + "b2"]
    lay["b1"] = A[f0 + "b1"].reshape(A[f0 + "b1"].shape[0], -1, 128).transpose(0, 2, 1)
    lay["w_exp"] = np.concatenate([A[f1 + "W_exp"], A[f1 + "b_exp"].reshape(1, -1)], 0).T
    lay["w_con"] = A[f1 + "W_con"]
    for k, name in (("up_w", "up_weights"), ("down_w", "down_weights")):
        lay[k] = A[f1 + name].reshape(*A[f1 + name].shape[:2], 4)
    lay["up_bias"] = per_channel(A[f1 + "up_bias"])
    lay["b_con"], lay["down_bias"] = A[f1 + "b_con"].reshape(1, -1), A[f1 + "down_bias"].reshape(1, -1)
    arrays, hbm = {}, {}
    for k, v in lay.items():
        arrays["in_" + k] = a = np.ascontiguousarray(v)
        hbm[k] = nc.dram_tensor("in_" + k, a.shape, mb.dt.from_np(a.dtype), kind="ExternalInput").ap()
    shape = A["L0_attn_hidden_states"].shape
    out = nc.dram_tensor("out", shape, mb.dt.float32, kind="ExternalOutput").ap()
    build(nc, hbm, out)
    got = run_bass_kernel_spmd(nc, [arrays], core_ids=[0])
    return got.results[0]["out"]
```

```python
import concourse.bass as bass
from concourse import mybir
from contextlib import ExitStack

FP32 = mybir.dt.float32
ALU = mybir.AluOpType
ACT = mybir.ActivationFunctionType
AX = mybir.AxisListType


def ge(engine, semaphore, value):
    if not isinstance(value, int) or value > 0:
        engine.wait_ge(semaphore, value)


def build(nc, hbm, out):
    P = 128
    B, L, D = hbm["L0_x"].shape
    DI, DCONV = hbm["L0_conv_w"].shape
    N = hbm["L0_A_log"].shape[1]
    C = DI // P
    K = D // P
    TT = L // P
    NT = B * TT
    RANKS = [hbm["L0_dt_w"].shape[0], hbm["L1_dt_w"].shape[0]]
    RMAX = max(RANKS)
    E, _, F = hbm["W1"].shape
    FB = F // P
    TS = 2 * P
    TR = TS // P
    SMAX = B * L // TS
    TILES = (B * L - E) // TS + E
    STAGES = hbm["up_w"].shape[0]
    NEAR = P.bit_length() - 1
    FAR = STAGES - NEAR
    EPS = 1e-5
    PAD = DCONV - 1

    ctx = ExitStack()
    with ctx:
        def sb(name, shape, dt=FP32):
            return ctx.enter_context(nc.sbuf_tensor(name, shape, dt))

        def sem(name):
            return ctx.enter_context(nc.semaphore(name))

        x = sb("x", [P, NT, D])
        ident = sb("ident", [P, P])
        w_in = sb("w_in", [P, K, 2 * DI])
        w_out = sb("w_out", [P, C, D])
        w_x = sb("w_x", [P, C, RMAX + 2 * N])
        w_dt = sb("w_dt", [2 * N + RMAX, DI])
        conv_w = sb("conv_w", [P, C, DCONV])
        a_log = sb("a_log", [P, C, N])
        a_neg = sb("a_neg", [P, C, N])
        chan = sb("chan", [P, 3, C])
        stats = sb("stats", [P, TT, 6])
        mv = sb("mv", [P, TT, 2])
        ve = sb("ve", [P, TT])
        rstd = sb("rstd", [P, TT])
        neg_half = sb("neg_half", [P, TT])
        shift = sb("shift", [P, TT])
        zero_row = sb("zero_row", [P, 1, D])
        up_b = sb("up_b", [P, FB])
        gelu_b = sb("gelu_b", [P, FB])
        w_top = sb("w_top", [P, NT])
        dest = sb("dest", [P, NT], mybir.dt.uint32)

        BCS, HS, AS = 4, 4, 4
        with ExitStack() as own:
            def sb1(name, shape, dt=FP32):
                return own.enter_context(nc.sbuf_tensor(name, shape, dt))
            xs = sb1("xs", [P, TT, D])
            xT = sb1("xT", [P, 2, K, L])
            xpad = sb1("xpad", [P, C, L + PAD])
            u = sb1("u", [P, 2, C, L])
            yz = sb1("yz", [P, C, L])
            delta = sb1("delta", [P, 2, C, L])
            du = sb1("du", [P, C, L])
            xd_row = sb1("xd_row", [2 * N + RMAX, L])
            b_row = sb1("b_row", [P, BCS, L])
            c_row = sb1("c_row", [P, BCS, L])
            hst = sb1("hst", [P, HS, C, L])
            dA = sb1("dA", [P, AS, C, L])
            prod = sb1("prod", [P, 2, C, L])

        I32 = mybir.dt.int32
        with ExitStack() as own:
            def sb2(name, shape, dt=FP32):
                return own.enter_context(nc.sbuf_tensor(name, shape, dt))
            before_m = sb2("before_m", [P, P])
            ones = sb2("ones", [P, P])
            prio = sb2("prio", [P, 1, E])
            steps = sb2("steps", [P, 1, SMAX])
            tile_no = sb2("tile_no", [P, TILES, 1])
            restart = sb2("restart", [P, E, NT])
            lg = sb2("lg", [P, NT, E])
            eq = sb2("eq", [P, NT, E])
            pick = sb2("pick", [P, NT, E])
            top = sb2("top", [P, NT])
            tot = sb2("tot", [P, E, NT])
            cum = sb2("cum", [P, E, NT])
            cmp_s = sb2("cmp_s", [P, E, SMAX])
            n_tiles = sb2("n_tiles", [P, E])
            end_tile = sb2("end_tile", [P, E])
            first_tile = sb2("first_tile", [P, E])
            cmp_t = sb2("cmp_t", [P, TILES, E])
            tile_e = sb2("tile_e", [P, TILES])
            tile_i = sb2("tile_i", [P, TILES], I32)
            dest_f = sb2("dest_f", [P, NT])
            w1 = sb2("w1", [P, 2, K, F])
            w2 = sb2("w2", [P, 2, FB, D])
            b1 = sb2("b1", [P, 2, FB])
            b2 = sb2("b2", [P, 2, D])
            xg = sb2("xg", [P, 2, TR, D])
            xgT = sb2("xgT", [P, K, TS])
            hid = sb2("hid", [P, FB, TS])
            yt = sb2("yt", [P, 2, TR, D])
            with ExitStack() as prep:
                def sb3(name, shape, dt=FP32):
                    return prep.enter_context(nc.sbuf_tensor(name, shape, dt))
                DA = D + 1
                bf_w = sb3("bf_w", [P, 2, 4 * F // 2])
                bf_m = sb3("bf_m", [P, 2, F])
                bf_t = sb3("bf_t", [P, 2, F])
                far_w = sb3("far_w", [P, 2, FAR, FB // 2, 4])
                w_exp = sb3("w_exp", [P, FB, DA])
                va = sb3("va", [P, FB, DA])
                vb = sb3("vb", [P, FB, DA])
                far_t = sb3("far_t", [P, 2, FB // 2, DA])
                m_T = sb3("m_T", [P, FB, P])
                gate_w = sb3("gate_w", [P, K, E])
                gate_b = sb3("gate_b", [P, 1, E])
                g_rows = sb3("g_rows", [P, 2, TT, D])
                g_cols = sb3("g_cols", [P, 2, K, L])

        with ExitStack() as own:
            def sb4(name, shape, dt=FP32):
                return own.enter_context(nc.sbuf_tensor(name, shape, dt))
            sb4("below", [P, TT * D + 2 * K * L + C * (L + PAD) + (2 + 1 + 2 + 1) * C * L + L + 2 * BCS * L])
            f_up = sb4("f_up", [P, K, F])
            f_down = sb4("f_down", [P, FB, D])
            f_bias = sb4("f_bias", [P, 2, D])
            f_rows = sb4("f_rows", [P, 2, TT, D])
            f_cols = sb4("f_cols", [P, K, L])
            f_hid = sb4("f_hid", [P, FB, L])

        yb = [ctx.enter_context(nc.psum_tensor(f"y{c}", [P, L], FP32)) for c in range(C)]
        pj = [ctx.enter_context(nc.psum_tensor(f"pj{i}", [P, L], FP32)) for i in range(4)]

        banks = yb + pj
        yg = prod[:, :, :, :].rearrange("p s c l -> p s (c l)")[:, :, 0:TT * D].rearrange("p s (i d) -> p s i d", d=D)

        x_sorted = nc.dram_tensor("x_sorted", [TILES * TS, D], FP32, kind="Internal").ap()
        y_sorted = nc.dram_tensor("y_sorted", [TILES * TS, D], FP32, kind="Internal").ap()
        up_dense = nc.dram_tensor("up_dense", [P, K * F], FP32, kind="Internal").ap()
        down_dense = nc.dram_tensor("down_dense", [P, FB * D], FP32, kind="Internal").ap()
        xdbl = nc.dram_tensor("xdbl_scratch", [2, 2 * N * L], FP32, kind="Internal").ap()

        x0_loaded, x_loaded, w_loaded = sem("x0_loaded"), sem("x_loaded"), sem("w_loaded")
        const_made, ident_made, pads_zeroed = sem("const_made"), sem("ident_made"), sem("pads_zeroed")
        a_exp, a_ready = sem("a_exp"), sem("a_ready")
        xs_loaded = sem("xs_loaded")
        xT_ps, xT_sb = sem("xT_ps"), sem("xT_sb")
        xin_ps, xin_sb = sem("xin_ps"), sem("xin_sb")
        conv_tap, u_ready = sem("conv_tap"), sem("u_ready")
        xdbl_ps, xdbl_sb, bc_stored = sem("xdbl_ps"), sem("xdbl_sb"), sem("bc_stored")
        b_loaded = [sem(f"b_loaded{i}") for i in range(BCS)]
        c_loaded = [sem(f"c_loaded{i}") for i in range(BCS)]
        dt_ps, dt_sb, sp_exp, ln_ready = sem("dt_ps"), sem("dt_sb"), sem("sp_exp"), sem("ln_ready")
        delta_ready, du_ready = sem("delta_ready"), sem("du_ready")
        z_ps, z_sb, zs_ready = sem("z_ps"), sem("z_sb"), sem("zs_ready")
        dA_ready, dbu_made, scan_done = sem("dA_ready"), sem("dbu_made"), sem("scan_done")
        prod_made, y_summed, y_free = sem("prod_made"), sem("y_summed"), sem("y_free")
        yz_ready, out_ps, res_done = sem("yz_ready"), sem("out_ps"), sem("res_done")
        stat_done, aggr_done, var_ready = sem("stat_done"), sem("aggr_done"), sem("var_ready")
        rstd_ready, norm_done = sem("rstd_ready"), sem("norm_done")
        shift_made, shift_free = sem("shift_made"), sem("shift_free")
        out_stored = sem("out_stored")
        waits_passed = sem("waits_passed")
        zero_made, sorted_zeroed = sem("zero_made"), sem("sorted_zeroed")
        gate_loaded, moe_const = sem("gate_loaded"), sem("moe_const")
        g_loaded = [sem("g_loaded0"), sem("g_loaded1")]
        g_rows_free, g_cols_free = sem("g_rows_free"), sem("g_cols_free")
        gT_ps, gT_sb = sem("gT_ps"), sem("gT_sb")
        route, gate_exp, picked, ranked, routed = (sem("route"), sem("gate_exp"), sem("picked"), sem("ranked"),
                                                   sem("routed"))
        scattered, gathered = sem("scattered"), [sem("gathered0"), sem("gathered1")]
        gathered_added = sem("gathered_added")
        xg_loaded = [sem("xg_loaded0"), sem("xg_loaded1")]
        w1_loaded = [sem("w1_loaded0"), sem("w1_loaded1")]
        w2_loaded = [sem("w2_loaded0"), sem("w2_loaded1")]
        y_stored = [sem("y_stored0"), sem("y_stored1")]
        yt_made = sem("yt_made")
        tT_ps, tT_sb, hid_ps, hid_sb, yt_ps = (sem("tT_ps"), sem("tT_sb"), sem("hid_ps"), sem("hid_sb"),
                                               sem("yt_ps"))
        bf_loaded = [sem("bf_loaded0"), sem("bf_loaded1")]
        bf_step, far_loaded, dense_loaded = sem("bf_step"), sem("far_loaded"), sem("dense_loaded")
        far_step, up_ps, up_sb, down_ps, down_sb = (sem("far_step"), sem("up_ps"), sem("up_sb"), sem("down_ps"),
                                                    sem("down_sb"))
        upT_ps, upT_sb, mT_ps, mT_sb, folded = sem("upT_ps"), sem("upT_sb"), sem("mT_ps"), sem("mT_sb"), sem("folded")
        far_part = sem("far_part")
        dense_stored, up_folded, down_folded = sem("dense_stored"), sem("up_folded"), sem("down_folded")
        f_loaded, f_rows_loaded = sem("f_loaded"), [sem("f_rows_loaded0"), sem("f_rows_loaded1")]
        f_rows_free, fT_ps, fT_sb = sem("f_rows_free"), sem("fT_ps"), sem("fT_sb")
        fh_ps, fh_sb, fy_ps, fy_free, f_added = (sem("fh_ps"), sem("fh_sb"), sem("fy_ps"), sem("fy_free"),
                                                 sem("f_added"))

        def half(t, b):
            flat = t[:, :, :, :].rearrange("p h c l -> p (h c l)")
            return flat[:, bass.ds((b % 2) * (C * L), C * L)]

        def chunk(t, b, c, skip=0):
            flat = t[:, :, :, :].rearrange("p h c l -> p (h c l)")
            return flat[:, bass.ds((b % 2) * (C * L) + c * L + skip, L - skip)]

        def columns(p, k):
            return xT[:, :, :, :].rearrange("p h k l -> p (h k l)")[:, bass.ds((p % 2) * (K * L) + k * L, L)]

        def over_batches(engine, before, body):
            before()
            body(0)
            with engine.Fori(1, B - 1) as b:
                body(b)
            body(B - 1)

        def is_first(b):
            return isinstance(b, int) and b == 0

        def is_last(b):
            return isinstance(b, int) and b == B - 1

        W_DMAS = 9
        FOLDS = 5
        AHEAD = 3

        SP_AT = dict(xs=4)
        POOL_AT = dict(deltas=15)
        PE_AT = dict(T=0, X=(0, 0, 1, 3), xdbl=(6, 6, 6, 6), dt=(7, 7, 8, 8), out=(1, 3, 3, 5), Z=(9, 10, 11, 11))
        ACT_AT = dict(xT=3, xin=(4, 4, 4, 6), u=10, xdbl=11, dt=(12, 12, 12, 12), sp=12, z=(13, 14, 14, 15), norm=14)
        DVE_AT = dict(conv=(3, 5), res=(9, 10), stats=11, shift=12, gate=1)

        block = ctx.enter_context(nc.Block())

        def ge_alone(engine, semaphore, value):
            if not isinstance(value, int) or value > 0:
                engine.wait_ge(semaphore, value)
                if not isinstance(value, int):
                    engine.sem_inc(waits_passed, 1)

        @block.sync
        def _(sp):
            def load_weights(lay):
                p = f"L{lay}_"
                R = RANKS[lay]
                for dst, src in (
                    (w_in[:, :, :], hbm[p + "w_in"].rearrange("(k p) e -> p k e", p=P)),
                    (w_x[:, :, 0:R + 2 * N], hbm[p + "w_x"].rearrange("(c p) r -> p c r", p=P)),
                    (w_dt[2 * N:2 * N + R, :], hbm[p + "dt_w"]),
                    (conv_w[:, :, :], hbm[p + "conv_w"].rearrange("(c p) k -> p c k", p=P)),
                    (a_log[:, :, :], hbm[p + "A_log"].rearrange("(c p) n -> p c n", p=P)),
                    (chan[:, 0, :], hbm[p + "conv_b"]),
                    (chan[:, 1, :], hbm[p + "dt_b"]),
                    (chan[:, 2, :], hbm[p + "D"]),
                    (w_out[:, :, :], hbm[p + "w_out"].rearrange("(c p) d -> p c d", p=P)),
                ):
                    sp.dma_start(dst, src).then_inc(w_loaded, 16)

            def load_xs(p):
                sp.dma_start(xs[:, :, :].rearrange("p i d -> p (i d)"),
                             x[:, bass.ds(p * TT, TT), :].rearrange("p i d -> p (i d)")).then_inc(xs_loaded, 16)

            def load_state_rows(lay):
                load_xs(0)
                if lay == 0:
                    sp.dma_start(x[:, TT:NT, :], rows[:, TT:NT, :]).then_inc(x_loaded, 16)
                    sp.wait_ge(zero_made, 1)
                    sp.dma_start(x_sorted.rearrange("(n p) d -> p n d", p=P),
                                 zero_row[:, :, :].broadcast_to([P, TILES * TR, D])).then_inc(sorted_zeroed, 16)
                sp.wait_ge(xT_ps, K * (lay * B + 1))
                if lay == 0:
                    sp.wait_ge(x_loaded, 16)
                else:
                    sp.wait_ge(norm_done, B + 2)
                load_xs(1)
                sp.wait_ge(bc_stored, 16 * (lay * B + 1))
                for n in range(AHEAD):
                    load_b(lay * B, n)
                batch(0, lay * B, True, True)
                with sp.Fori(1, B - 2) as b:
                    batch(b, b + lay * B, True, True)
                batch(B - 2, B - 2 + lay * B, False, True)
                batch(B - 1, B - 1 + lay * B, False, False)

            def row(g, i, ring, n):
                src = xdbl[bass.ds(g % 2, 1), bass.ds(i * L, L)]
                return sp.dma_start(ring[:, n % BCS, :], src.broadcast_to([P, L]))

            def load_b(g, n):
                ge(sp, dbu_made, N * g + n - BCS + 1)
                row(g, 2 * n, b_row, n).then_inc(b_loaded[n % BCS], 16)

            def load_c(g, n):
                ge(sp, prod_made, N * g + n - BCS + 1)
                row(g, 2 * n + 1, c_row, n).then_inc(c_loaded[n % BCS], 16)

            def batch(b, g, load_rows, has_next):
                for n in range(N):
                    if load_rows and n == SP_AT["xs"]:
                        sp.wait_ge(xT_ps, K * (g + 2))
                        load_xs(b + 2)
                    if n + AHEAD < N:
                        load_b(g, n + AHEAD)
                    elif has_next:
                        if n + AHEAD == N:
                            sp.wait_ge(bc_stored, 16 * (g + 2))
                        load_b(g + 1, n + AHEAD - N)
                    load_c(g, n)

            def batch_rows(p):
                return x[:, bass.ds(p * TT, TT), :].rearrange("p i d -> p (i d)")

            def load_gate_rows():
                with sp.Fori(0, B // 2) as h:
                    for s in range(2):
                        ge_alone(sp, norm_done, 2 * h + s + 1)
                        sp.wait_ge(g_rows_free, 2 * h + s + 1)
                        sp.dma_start(g_rows[:, s, :, :].rearrange("p i d -> p (i d)"),
                                     batch_rows(2 * h + s)).then_inc(g_loaded[s], 16)

            def load_rows(j, s):
                sp.dma_start(xg[:, s, :, :], x_sorted[bass.ds(j * TS, TS), :].rearrange("(r p) d -> p r d", p=P)
                             ).then_inc(xg_loaded[s], 16)

            def load_expert(j, s, first):
                e = sp.value_load(tile_i[0:1, bass.ds(j, 1)], min_val=0, max_val=E - 1)
                if not first:
                    ge_alone(sp, hid_ps, FB // 2 * (j - 1))
                    ge_alone(sp, hid_sb, FB // 2 * (j - 1))
                for dst, src in (
                    (w1[:, s, :, :], hbm["W1"][bass.ds(e, 1), :, :].rearrange("o (k p) f -> p (o k) f", p=P)),
                    (b1[:, s, :], hbm["b1"][bass.ds(e, 1), :, :].rearrange("o p f -> p (o f)")),
                ):
                    sp.dma_start(dst, src).then_inc(w1_loaded[s], 16)
                if not first:
                    ge_alone(sp, yt_ps, j - 1)
                    ge_alone(sp, yt_made, j + 1)
                for dst, src in (
                    (w2[:, s, :, :], hbm["W2"][bass.ds(e, 1), :, :].rearrange("o (f p) d -> p (o f) d", p=P)),
                    (b2[:, s, :], hbm["b2"][bass.ds(e, 1), :].broadcast_to([P, D])),
                ):
                    sp.dma_start(dst, src).then_inc(w2_loaded[s], 16)

            def load_tile(j, s):
                ge_alone(sp, tT_ps, j - 1)
                load_rows(j, s)
                load_expert(j, s, False)

            def store_tile(j, s):
                sp.wait_ge(yt_made, j + 3)
                sp.dma_start(y_sorted[bass.ds(j * TS, TS), :].rearrange("(r p) d -> p r d", p=P),
                             yt[:, s, :, :]).then_inc(y_stored[s], 16)

            def experts():
                sp.wait_ge(prod_made, N * B)
                for dst, src in (
                    (gate_w[:, :, :], hbm["gate_w"].rearrange("(k p) e -> p k e", p=P)),
                    (gate_b[:, 0, :], hbm["gate_b"].broadcast_to([P, E])),
                ):
                    sp.dma_start(dst, src).then_inc(gate_loaded, 16)
                load_gate_rows()
                for dst, src in (
                    (far_w[:, 0, :, :, :], hbm["up_w"][NEAR:STAGES, :, :].rearrange("s (q p) w -> p s q w", p=P)),
                    (far_w[:, 1, :, :, :], hbm["down_w"][NEAR:STAGES, :, :].rearrange("s (q p) w -> p s q w", p=P)),
                    (va[:, :, 0:D], hbm["w_con"].rearrange("(f p) d -> p f d", p=P)),
                    (up_b[:, :], hbm["up_bias"]),
                ):
                    sp.dma_start(dst, src).then_inc(far_loaded, 16)
                sp.dma_start(w_exp[:, :, :], hbm["w_exp"].rearrange("(f p) d -> p f d", p=P)).then_inc(dense_loaded, 16)
                load_weights(1)
                sp.wait_ge(routed, 1)
                load_expert(0, 0, True)
                load_expert(1, 1, True)
                sp.wait_ge(scattered, 16 * NT)
                load_rows(0, 0)
                load_rows(1, 1)
                with sp.Fori(1, TILES // 2) as h:
                    for s in range(2):
                        load_tile(2 * h + s, s)
                        store_tile(2 * h + s - 2, s)
                load_tile(TILES - 1, 0)
                for j in (TILES - 3, TILES - 2, TILES - 1):
                    store_tile(j, j % 2)
                sp.wait_ge(down_folded, 1)
                sp.dma_start(down_dense, bf_m[:, :, :].rearrange("p a f -> p (a f)")).then_inc(dense_stored, 16)
                sp.wait_ge(up_folded, 1)
                sp.dma_start(up_dense, bf_t[:, :, :].rearrange("p a f -> p (a f)")).then_inc(dense_stored, 16)

            def last_layer():
                sp.wait_ge(prod_made, 2 * N * B)
                for dst, src in (
                    (f_up[:, :, :].rearrange("p k f -> p (k f)"), up_dense),
                    (f_down[:, :, :].rearrange("p f d -> p (f d)"), down_dense),
                    (f_bias[:, 0, :], hbm["b_con"].broadcast_to([P, D])),
                    (f_bias[:, 1, :], hbm["down_bias"].broadcast_to([P, D])),
                ):
                    sp.dma_start(dst, src).then_inc(f_loaded, 16)
                with sp.Fori(0, B // 2) as h:
                    for s in range(2):
                        ge_alone(sp, norm_done, 2 * B + 2 * h + s + 1)
                        sp.wait_ge(f_rows_free, 2 * h + s + 1)
                        sp.dma_start(f_rows[:, s, :, :].rearrange("p i d -> p (i d)"),
                                     batch_rows(2 * h + s)).then_inc(f_rows_loaded[s], 16)

            rows = hbm["L0_x"].rearrange("b (i p) d -> p (b i) d", p=P)
            sp.dma_start(x[:, 0:TT, :], rows[:, 0:TT, :]).then_inc(x0_loaded, 16)
            load_weights(0)
            sp.wait_ge(x0_loaded, 16)
            load_state_rows(0)
            experts()
            sp.wait_ge(norm_done, B + 1)
            sp.wait_ge(dense_stored, 32)
            load_state_rows(1)
            last_layer()

        @block.gpsimd
        def _(pool):
            nc.gpsimd.memset(neg_half[:, :], -0.5).then_inc(const_made, 1)
            nc.gpsimd.memset(ident[:, :], 0.0).then_inc(const_made, 1)
            nc.gpsimd.memset(zero_row[:, :, :], 0.0).then_inc(zero_made, 1)
            pool.wait_ge(const_made, 2)
            nc.gpsimd.affine_select(out=ident[:, :], in_=ident[:, :], compare_op=ALU.not_equal, fill=1.0,
                                    base=0, pattern=[[-1, P]], channel_multiplier=1).then_inc(ident_made, 1)

            def norm_power(q):
                pool.wait_ge(var_ready, q + 1)
                nc.gpsimd.tensor_tensor(out=rstd[:, :], in0=ve[:, :], in1=neg_half[:, :],
                                        op=ALU.pow).then_inc(rstd_ready, 1)

            def deltas(p, g):
                ge_alone(pool, ln_ready, g + 1)
                d3 = half(delta, p).rearrange("p (c l) -> p c l", c=C)
                nc.gpsimd.tensor_tensor(out=d3, in0=d3, in1=xpad[:, :, PAD:PAD + L],
                                        op=ALU.add).then_inc(delta_ready, 1)

            def mamba(lay):
                def body(b):
                    g = b + lay * B
                    for n in range(N):
                        if n == 0:
                            ge_alone(pool, delta_ready, g + 1)
                            ge_alone(pool, u_ready, g + 1)
                            ge_alone(pool, dbu_made, N * g)
                            nc.gpsimd.tensor_tensor(out=du[:, :, :].rearrange("p c l -> p (c l)"), in0=half(delta, b),
                                                    in1=half(u, b), op=ALU.mult).then_inc(du_ready, 1)
                            ge_alone(pool, du_ready, g + 1)
                        ge_alone(pool, b_loaded[n % BCS], 16 * (N // BCS * g + n // BCS + 1))
                        ge_alone(pool, prod_made, N * g + n - HS + 1)
                        nc.gpsimd.tensor_tensor(
                            out=hst[:, n % HS, :, :],
                            in0=du[:, :, :],
                            in1=b_row[:, n % BCS:n % BCS + 1, :].broadcast_to([P, C, L]),
                            op=ALU.mult).then_inc(dbu_made, 1)
                        if n == POOL_AT["deltas"] and not is_last(b):
                            deltas(b + 1, g + 1)
                    if not is_first(b):
                        norm_power(g - 1 + lay * B)

                over_batches(pool, lambda: None, body)
                norm_power(2 * lay * B + B - 1)

            def experts():
                pool.wait_ge(norm_done, B)
                nc.gpsimd.memset(before_m[:, :], 1.0).then_inc(moe_const, 1)
                nc.gpsimd.memset(ones[:, :], 1.0).then_inc(moe_const, 1)
                nc.gpsimd.memset(restart[:, :, :], 1.0).then_inc(moe_const, 1)
                pool.wait_ge(moe_const, 3)
                nc.gpsimd.affine_select(out=before_m[:, :], in_=before_m[:, :], compare_op=ALU.is_gt, fill=0.0,
                                        base=0, pattern=[[1, P]], channel_multiplier=-1).then_inc(moe_const, 1)
                nc.gpsimd.memset(restart[:, :, 0:1], 0.0).then_inc(moe_const, 1)
                for t, pattern, base in ((prio, [[-1, E]], E), (steps, [[TS, SMAX]], 0), (tile_no, [[1, TILES]], 0)):
                    nc.gpsimd.iota(t[:, :, :].rearrange("p a b -> p (a b)"), pattern=pattern, base=base,
                                   channel_multiplier=0,
                                   allow_small_or_imprecise_dtypes=True).then_inc(moe_const, 1)
                pool.wait_ge(sorted_zeroed, 16)
                pool.wait_ge(routed, 1)
                for t in range(NT):
                    nc.gpsimd.indirect_dma_start(
                        out=x_sorted, out_offset=bass.IndirectOffsetOnAxis(ap=dest[:, t:t + 1], axis=0),
                        in_=x[:, t, :], in_offset=None).then_inc(scattered, 16)
                near_butterflies()
                for s in range(2):
                    pool.wait_ge(y_stored[s], 16 * ((TILES + 1 - s) // 2))
                gather(0)
                gather(1)
                for e in range(B):
                    norm_power(B + e)
                    if e + 2 < B:
                        pool.wait_ge(gathered_added, e + 1)
                        gather(e + 2)

            def gather(e):
                for i in range(TT):
                    t = e * TT + i
                    nc.gpsimd.indirect_dma_start(
                        out=yg[:, e % 2, i, :], out_offset=None,
                        in_=y_sorted, in_offset=bass.IndirectOffsetOnAxis(ap=dest[:, t:t + 1], axis=0)
                        ).then_inc(gathered[e % 2], 16)

            def near_butterflies():
                done = 0
                for half_, name in enumerate(("up_w", "down_w")):
                    for b in range(FB):
                        nc.gpsimd.tensor_copy(bf_m[:, half_, b * P:(b + 1) * P], ident[:, :]).then_inc(bf_step, 1)
                    done += FB
                    for stage in range(NEAR):
                        i = half_ * NEAR + stage
                        st = 1 << stage
                        if stage == 0:
                            load_near(name, 0, i)
                        pool.wait_ge(bf_step, done)
                        if stage + 1 < NEAR:
                            load_near(name, stage + 1, i + 1)
                        pool.wait_ge(bf_loaded[i % 2], 16 * (i // 2 + 1))
                        m = bf_m[:, half_, :].rearrange("p (n two s) -> p n two s", two=2, s=st)
                        w = bf_w[:, i % 2, :].rearrange("p (n s r c) -> p n r s c", s=st, r=2, c=2)
                        o = [bf_t[:, t, :].rearrange("p (n r s) -> p n r s", r=2, s=st) for t in range(2)]
                        shape = [P, F // (2 * st), 2, st]
                        for col in range(2):
                            nc.gpsimd.tensor_tensor(out=o[col], in0=w[:, :, :, :, col],
                                                    in1=m[:, :, col:col + 1, :].broadcast_to(shape),
                                                    op=ALU.mult).then_inc(bf_step, 1)
                        done += 2
                        pool.wait_ge(bf_step, done)
                        nc.gpsimd.tensor_tensor(out=bf_m[:, half_, :], in0=bf_t[:, 0, :], in1=bf_t[:, 1, :],
                                                op=ALU.add).then_inc(bf_step, 1)
                        done += 1
                pool.wait_ge(bf_step, done)
                pool.sem_inc(folded, 1)

            def load_near(name, stage, i):
                w = hbm[name][stage:stage + 1, :, :].rearrange("s k w -> s (k w)")
                pool.dma_start(bf_w[:, i % 2, :], w.broadcast_to([P, 4 * F // 2])).then_inc(bf_loaded[i % 2], 16)

            def last_layer():
                def store(p):
                    norm_power(3 * B + p)
                    ge_alone(pool, norm_done, 3 * B + p + 1)
                    pool.dma_start(out.rearrange("b (i p) d -> p (b i) d", p=P)[:, bass.ds(p * TT, TT), :],
                                   x[:, bass.ds(p * TT, TT), :]).then_inc(out_stored, 16)
                with pool.Fori(0, B) as p:
                    store(p)
                pool.wait_ge(out_stored, 16 * B)

            mamba(0)
            experts()
            mamba(1)
            last_layer()

        @block.scalar
        def _(act):
            def pre_xT(p, g):
                for k in range(K):
                    ge_alone(act, xT_ps, K * g + k + 1)
                    if k == 0:
                        ge_alone(act, z_ps, C * (g - 1))
                    nc.scalar.activation(columns(p, k), pj[k][:, :], ACT.Copy).then_inc(xT_sb, 1)

            def pre_xin(p, g, c):
                ge_alone(act, xin_ps, C * g + c + 1)
                if c == 0:
                    ge_alone(act, delta_ready, g)
                    ge_alone(act, yz_ready, g - 1)
                bank = pj[(c + 2) % 4]
                nc.scalar.activation(xpad[:, c, PAD:PAD + L], bank[:, :], ACT.Copy)
                nc.scalar.activation(chunk(u, p, c), bank[:, :], ACT.Identity,
                                     scale=conv_w[:, c, PAD:PAD + 1]).then_inc(xin_sb, 1)

            def pre_u(p, g):
                ge_alone(act, conv_tap, C * PAD * (g + 1))
                for c in range(C):
                    i = nc.scalar.activation(chunk(u, p, c), chunk(u, p, c), ACT.Silu, bias=chan[:, 0, c:c + 1])
                i.then_inc(u_ready, 1)

            def pre_xdbl(p, g, R):
                ge_alone(act, xdbl_ps, g + 1)
                ge_alone(act, bc_stored, 16 * g)
                ge_alone(act, dt_ps, C * g)
                nc.scalar.activation(xd_row[0:2 * N + R, :], pj[0][0:2 * N + R, :], ACT.Copy).then_inc(xdbl_sb, 1)
                ge_alone(act, xdbl_sb, g + 1)
                ge_alone(act, dbu_made, N * (g - 1))
                ge_alone(act, prod_made, N * (g - 1))
                act.dma_start(xdbl[bass.ds(p % 2, 1), :].rearrange("o (r l) -> (o r) l", l=L),
                              xd_row[0:2 * N, :]).then_inc(bc_stored, 16)

            def pre_dt(p, g, c):
                ge_alone(act, dt_ps, C * g + c + 1)
                if c == 0:
                    ge_alone(act, du_ready, g - 1)
                    ge_alone(act, dA_ready, N * (g - 1))
                nc.scalar.activation(xpad[:, c, PAD:PAD + L], pj[c % 2][:, :], ACT.Abs,
                                     bias=chan[:, 1, c:c + 1])
                nc.scalar.activation(chunk(delta, p, c), pj[c % 2][:, :], ACT.Relu,
                                     bias=chan[:, 1, c:c + 1]).then_inc(dt_sb, 1)

            def pre_softplus(p, g):
                ge_alone(act, dt_sb, C * g + C)
                nc.scalar.activation(xpad[:, :, PAD:PAD + L], xpad[:, :, PAD:PAD + L], ACT.Exp,
                                     scale=-1.0).then_inc(sp_exp, 1)
                ge_alone(act, sp_exp, g + 1)
                nc.scalar.activation(xpad[:, :, PAD:PAD + L], xpad[:, :, PAD:PAD + L], ACT.Ln,
                                     bias=1.0).then_inc(ln_ready, 1)

            def gate_z(g, lo, hi):
                for c in range(lo, hi):
                    ge_alone(act, z_ps, C * g + c + 1)
                    if c == 0:
                        ge_alone(act, out_ps, 2 * g)
                    nc.scalar.activation(yz[:, c, :], pj[2 + c % 2][:, :], ACT.Copy).then_inc(z_sb, 1)
                if hi == C:
                    ge_alone(act, z_sb, C * (g + 1))
                    nc.scalar.activation(yz[:, :, :], yz[:, :, :], ACT.Silu).then_inc(zs_ready, 1)

            def normalise(e, shifts, norms):
                ge_alone(act, shift_made, shifts)
                for i in range(TT):
                    row = x[:, bass.ds(e * TT + i, 1), :].rearrange("p o d -> p (o d)")
                    a = nc.scalar.activation(row, row, ACT.Identity, scale=rstd[:, i:i + 1],
                                             bias=shift[:, i:i + 1])
                a.then_inc(norm_done, 1)
                ge_alone(act, norm_done, norms)
                act.sem_inc(shift_free, 1)

            def mamba(lay):
                R = RANKS[lay]

                def before():
                    act.wait_ge(w_loaded, 16 * W_DMAS * (lay + 1))
                    ge_alone(act, a_ready, lay)
                    nc.scalar.activation(a_neg[:, :, :], a_log[:, :, :], ACT.Exp).then_inc(a_exp, 1)
                    g = lay * B
                    act.wait_ge(pads_zeroed, lay + 1)
                    pre_xT(0, g)
                    for c in range(C):
                        pre_xin(0, g, c)
                    pre_u(0, g)
                    pre_xdbl(0, g, R)
                    for c in range(C):
                        pre_dt(0, g, c)
                    pre_softplus(0, g)
                    act.wait_ge(a_ready, lay + 1)

                def body(b):
                    g = b + lay * B
                    for n in range(N):
                        if n == 0:
                            ge_alone(act, delta_ready, g + 1)
                        ge_alone(act, scan_done, N * g + n - AS + 1)
                        for c in range(C):
                            i = nc.scalar.activation(dA[:, n % AS, c, 1:L], chunk(delta, b, c, 1), ACT.Exp,
                                                     scale=a_neg[:, c, n:n + 1])
                        i.then_inc(dA_ready, 1)
                        if not is_last(b):
                            if n == ACT_AT["xT"]:
                                pre_xT(b + 1, g + 1)
                            for c in range(C):
                                if n == ACT_AT["xin"][c]:
                                    pre_xin(b + 1, g + 1, c)
                            if n == ACT_AT["u"]:
                                pre_u(b + 1, g + 1)
                            if n == ACT_AT["xdbl"]:
                                pre_xdbl(b + 1, g + 1, R)
                            for c in range(C):
                                if n == ACT_AT["dt"][c]:
                                    pre_dt(b + 1, g + 1, c)
                            if n == ACT_AT["sp"]:
                                pre_softplus(b + 1, g + 1)
                        for c in range(C):
                            if n == ACT_AT["z"][c]:
                                gate_z(g, c, c + 1)
                        if not is_first(b) and n == ACT_AT["norm"]:
                            normalise(b - 1, b + lay * (B - 1), g + lay * B)

                over_batches(act, before, body)

            def experts():
                with act.Fori(0, B // 2) as h:
                    for s in range(2):
                        p = 2 * h + s
                        act.wait_ge(g_cols_free, p + 1)
                        for k in range(K):
                            act.wait_ge(gT_ps, K * p + k + 1)
                            nc.scalar.activation(g_cols[:, s, k, :], banks[2 * s + k][:, :], ACT.Copy
                                                 ).then_inc(gT_sb, 1)
                act.wait_ge(route, 3)
                nc.scalar.activation(eq[:, :, :], eq[:, :, :], ACT.Exp).then_inc(gate_exp, 1)

                def columns_of(j, s):
                    act.wait_ge(tT_ps, j + 1)
                    nc.scalar.activation(xgT[:, :, :].rearrange("p k t -> p (k t)"), banks[s][:, :], ACT.Copy
                                         ).then_inc(tT_sb, 1)

                def tile(j, s, last):
                    if not is_first(j):
                        act.wait_ge(yt_ps, j)
                    for q in range(FB // 2):
                        act.wait_ge(hid_ps, FB // 2 * j + q + 1)
                        for f in (2 * q, 2 * q + 1):
                            i = nc.scalar.activation(hid[:, f, :], banks[2 + q][:, (f % 2) * TS:(f % 2 + 1) * TS],
                                                     ACT.Silu, bias=b1[:, s, f:f + 1])
                        i.then_inc(hid_sb, 1)
                    if not last:
                        columns_of(j + 1, 1 - s)

                columns_of(0, 0)
                tile(0, 0, False)
                tile(1, 1, False)
                with act.Fori(1, (TILES - FOLDS) // 2) as h:
                    for s in range(2):
                        tile(2 * h + s, s, False)
                tile(TILES - 5, 0, False)
                for q in range(2):
                    act.wait_ge(mT_ps, q + 1)
                    nc.scalar.activation(m_T[:, 4 * q:4 * q + 4, :].rearrange("p b f -> p (b f)"), banks[2 + q][:, :],
                                         ACT.Copy).then_inc(mT_sb, 1)
                tile(TILES - 4, 1, False)
                for b in range(FB):
                    if b == 4:
                        tile(TILES - 3, 0, False)
                    act.wait_ge(up_ps, b + 1)
                    if b == 0:
                        act.wait_ge(far_step, 9)
                    nc.scalar.activation(va[:, b, :], banks[2 + b % 4][:, 0:DA], ACT.Copy).then_inc(up_sb, 1)
                tile(TILES - 2, 1, False)
                dst = bf_m[:, :, :].rearrange("p a f -> p (a f)")
                for q in range(FB // 2):
                    act.wait_ge(down_ps, q + 1)
                    nc.scalar.activation(dst[:, 2 * q * D:2 * (q + 1) * D], banks[2 + q][:, :], ACT.Copy
                                         ).then_inc(down_sb, 1)
                act.wait_ge(down_sb, FB // 2)
                act.sem_inc(down_folded, 1)
                tile(TILES - 1, 0, True)
                for q in range(FB // 2):
                    act.wait_ge(upT_ps, q + 1)
                    nc.scalar.activation(
                        bf_t[:, :, 2 * q * P:2 * (q + 1) * P].rearrange("p k (b f) -> p k b f", b=2),
                        banks[2 + q][:, :].rearrange("p (b k f) -> p k b f", b=2, k=K), ACT.Copy).then_inc(upT_sb, 1)
                act.wait_ge(upT_sb, FB // 2)
                act.sem_inc(up_folded, 1)

            def last_layer():
                act.wait_ge(f_loaded, 64)
                def take_columns(p):
                    for k in range(K):
                        act.wait_ge(fT_ps, K * p + k + 1)
                        nc.scalar.activation(f_cols[:, k, :], banks[k][:, :], ACT.Copy).then_inc(fT_sb, 1)

                def hidden(p):
                    for f in range(FB):
                        act.wait_ge(fh_ps, FB * p + f + 1)
                        if f == 0 and (not isinstance(p, int) or p > 0):
                            act.wait_ge(fy_ps, 2 * p)
                        nc.scalar.activation(f_hid[:, f, :], banks[2 + f % 4][:, :], ACT.Gelu,
                                             bias=gelu_b[:, f:f + 1]).then_inc(fh_sb, 1)

                take_columns(0)
                hidden(0)
                with act.Fori(1, B) as p:
                    take_columns(p)
                    hidden(p)

            mamba(0)
            experts()
            mamba(1)
            last_layer()

        @block.tensor
        def _(pe):
            pe.wait_ge(ident_made, 1)

            def pre_T(p, g):
                ge(pe, xs_loaded, 16 * (g + 1))
                for k in range(K):
                    ge(pe, dt_sb, C * g - 1 + k)
                    for i in range(TT):
                        t = nc.tensor.transpose(pj[k][:, i * P:(i + 1) * P],
                                                xs[:, i, k * P:(k + 1) * P], ident[:, :])
                    t.then_inc(xT_ps, 1)

            def pre_X(p, g, c):
                if c == 0:
                    ge(pe, xT_sb, K * (g + 1))
                if c < 2:
                    ge(pe, z_sb, C * (g - 1) - 1 + c)
                for k in range(K):
                    i = nc.tensor.matmul(pj[(c + 2) % 4][:, :], w_in[:, k, c * P:(c + 1) * P], columns(p, k),
                                         start=(k == 0), stop=(k == K - 1))
                i.then_inc(xin_ps, 1)

            def pre_xdbl(p, g, R, c):
                if c == 0:
                    ge(pe, u_ready, g + 1)
                i = nc.tensor.matmul(pj[0][0:2 * N + R, :], w_x[:, c, 0:2 * N + R], chunk(u, p, c),
                                     start=(c == 0), stop=(c == C - 1))
                if c == C - 1:
                    i.then_inc(xdbl_ps, 1)

            def pre_dt(p, g, R, c):
                low = slice(2 * N, 2 * N + R)
                if c == 0:
                    ge(pe, xdbl_sb, g + 1)
                if c >= 2:
                    ge(pe, dt_sb, C * g + c - 1)
                nc.tensor.matmul(pj[c % 2][:, :], w_dt[low, c * P:(c + 1) * P], xd_row[low, :],
                                 start=True, stop=True).then_inc(dt_ps, 1)

            def gate_Z(p, g, c):
                if c < 2:
                    ge(pe, res_done, 2 * g - 1 + c)
                else:
                    ge(pe, z_sb, C * g + c - 1)
                for k in range(K):
                    i = nc.tensor.matmul(pj[2 + c % 2][:, :], w_in[:, k, DI + c * P:DI + (c + 1) * P],
                                         columns(p, k),
                                         start=(k == 0), stop=(k == K - 1))
                i.then_inc(z_ps, 1)

            def project(g, i, interleaved):
                if i == 0:
                    ge(pe, yz_ready, g + 1)
                if i % 2 == 0:
                    if interleaved:
                        ge(pe, xin_sb, C * (g + 2) + 1 + i // 2)
                    else:
                        ge(pe, z_sb, C * (g + 1))
                bank = pj[2 + i // 2][:, (i % 2) * D:(i % 2 + 1) * D]
                for c in range(C):
                    lhsT = yz[:, c, i * P:(i + 1) * P]
                    m = nc.tensor.matmul(bank, lhsT, w_out[:, c, :], start=(c == 0), stop=(c == C - 1))
                if i % 2 == 1:
                    m.then_inc(out_ps, 1)

            def mamba(lay):
                R = RANKS[lay]

                def before():
                    g = lay * B
                    pe.wait_ge(w_loaded, 16 * W_DMAS * (lay + 1))
                    if lay == 0:
                        pe.wait_ge(x0_loaded, 16)
                    pre_T(0, g)
                    for c in range(C):
                        pre_X(0, g, c)
                    for c in range(C):
                        pre_xdbl(0, g, R, c)
                    for c in range(C):
                        pre_dt(0, g, R, c)

                def body(b):
                    g = b + lay * B
                    for n in range(N):
                        ge(pe, prod_made, N * g + n + 1)
                        for c in range(C):
                            if n == 0:
                                ge(pe, y_free, C * (g - 1) + c + 1)
                            i = nc.tensor.matmul(yb[c][:, :], ident[:, :], prod[:, n % 2, c, :],
                                                 start=(n == 0), stop=(n == N - 1))
                        i.then_inc(y_summed, 1)
                        if not is_last(b):
                            if n == PE_AT["T"]:
                                pre_T(b + 1, g + 1)
                            for c in range(C):
                                if n == PE_AT["X"][c]:
                                    pre_X(b + 1, g + 1, c)
                                if n == PE_AT["xdbl"][c]:
                                    pre_xdbl(b + 1, g + 1, R, c)
                            for c in range(C):
                                if n == PE_AT["dt"][c]:
                                    pre_dt(b + 1, g + 1, R, c)
                        for i in range(TT):
                            if not is_first(b) and n == PE_AT["out"][i]:
                                project(g - 1, i, not is_last(b))
                        for c in range(C):
                            if n == PE_AT["Z"][c]:
                                gate_Z(b, g, c)

                over_batches(pe, before, body)
                if lay == 1:
                    pe.sem_inc(f_rows_free, 2)
                    pe.wait_ge(f_loaded, 64)
                    pe.wait_ge(y_free, 2 * C * B)
                    rows_T(0, 0)
                for i in range(TT):
                    project(lay * B + B - 1, i, False)

            def experts():
                pe.wait_ge(y_free, C * B)
                pe.sem_inc(g_rows_free, 2)
                pe.sem_inc(g_cols_free, 2)
                pe.wait_ge(gate_loaded, 32)
                def gate_T(s, h):
                    pe.wait_ge(g_loaded[s], 16 * (h + 1))
                    for k in range(K):
                        for i in range(TT):
                            t = nc.tensor.transpose(banks[2 * s + k][:, i * P:(i + 1) * P],
                                                    g_rows[:, s, i, k * P:(k + 1) * P], ident[:, :])
                        t.then_inc(gT_ps, 1)

                def gate_logits(p, s):
                    pe.wait_ge(gT_sb, K * (p + 1))
                    pe.sem_inc(g_rows_free, 1)
                    for i in range(TT):
                        for k in range(K):
                            m = nc.tensor.matmul(pj[0][:, bass.ds((p * TT + i) * E, E)],
                                                 g_cols[:, s, k, i * P:(i + 1) * P], gate_w[:, k, :],
                                                 start=(k == 0), stop=(k == K - 1))
                    m.then_inc(g_cols_free, 1)

                gate_T(0, 0)
                with pe.Fori(0, B // 2 - 1) as h:
                    gate_T(1, h)
                    gate_logits(2 * h, 0)
                    gate_T(0, h + 1)
                    gate_logits(2 * h + 1, 1)
                gate_T(1, B // 2 - 1)
                gate_logits(B - 2, 0)
                gate_logits(B - 1, 1)
                pe.wait_ge(moe_const, 8)
                pe.wait_ge(picked, 1)
                flat = pick[:, :, :].rearrange("p t e -> p (t e)")
                nc.tensor.matmul(pj[1][:, 0:NT * E], before_m[:, :], flat, start=True, stop=True)
                nc.tensor.matmul(pj[2][:, 0:NT * E], ones[:, :], flat, start=True, stop=True).then_inc(ranked, 1)

                def tile_T(s, h):
                    pe.wait_ge(xg_loaded[s], 16 * (h + 1))
                    for k in range(K):
                        for r in range(TR):
                            t = nc.tensor.transpose(banks[s][:, k * TS + r * P:k * TS + (r + 1) * P],
                                                    xg[:, s, r, k * P:(k + 1) * P], ident[:, :])
                    t.then_inc(tT_ps, 1)

                def tile(j, s, h, last, fold_out=None, fold_before=0, fold_pieces=FB):
                    pe.wait_ge(tT_sb, j + 1)
                    pe.wait_ge(w1_loaded[s], 32 * (h + 1))
                    for f in range(FB):
                        if f % 2 == 0 and (not isinstance(j, int) or j > 0):
                            pe.wait_ge(hid_sb, FB // 2 * (j - 1) + f // 2 + 1)
                            if fold_out is not None:
                                pe.wait_ge(fold_out, min(fold_before + f // 2 + 1, fold_pieces))
                        for k in range(K):
                            m = nc.tensor.matmul(banks[2 + f // 2][:, (f % 2) * TS:(f % 2 + 1) * TS],
                                                 w1[:, s, k, f * P:(f + 1) * P], xgT[:, k, :],
                                                 start=(k == 0), stop=(k == K - 1))
                        if f % 2:
                            m.then_inc(hid_ps, 1)
                    if not last:
                        tile_T(1 - s, h + s)
                    pe.wait_ge(w2_loaded[s], 32 * (h + 1))
                    pe.wait_ge(yt_made, j + 1)
                    for r in range(TR):
                        for f in range(FB):
                            if r == 0 and f % 2 == 0:
                                pe.wait_ge(hid_sb, FB // 2 * j + f // 2 + 1)
                            m = nc.tensor.matmul(banks[6 + s][:, r * D:(r + 1) * D],
                                                 hid[:, f, r * P:(r + 1) * P], w2[:, s, f, :],
                                                 start=(f == 0), stop=(f == FB - 1))
                    m.then_inc(yt_ps, 1)

                tile_T(0, 0)
                tile(0, 0, 0, False)
                tile(1, 1, 0, False)
                with pe.Fori(1, (TILES - FOLDS) // 2) as h:
                    for s in range(2):
                        tile(2 * h + s, s, h, False)
                h = TILES // 2
                tile(TILES - 5, 0, h - 2, False)
                pe.wait_ge(folded, 1)
                for b in range(FB):
                    t = nc.tensor.transpose(banks[2 + b // 4][:, (b % 4) * P:(b % 4 + 1) * P],
                                            bf_m[:, 1, b * P:(b + 1) * P], ident[:, :])
                    if b % 4 == 3:
                        t.then_inc(mT_ps, 1)
                tile(TILES - 4, 1, h - 2, False, mT_sb, 0, 2)
                pe.wait_ge(dense_loaded, 16)
                fold_up(0)
                tile(TILES - 3, 0, h - 1, False, up_sb, 0)
                fold_up(4)
                tile(TILES - 2, 1, h - 1, False, up_sb, 4)
                pe.wait_ge(far_step, 9)
                for b in range(FB):
                    m = nc.tensor.matmul(banks[2 + b // 2][:, (b % 2) * D:(b % 2 + 1) * D], m_T[:, b, :],
                                         vb[:, b, 0:D], start=True, stop=True)
                    if b % 2:
                        m.then_inc(down_ps, 1)
                tile(TILES - 1, 0, h, True, down_sb, 0)
                pe.wait_ge(far_step, 18)
                for b in range(FB):
                    for k in range(K):
                        t = nc.tensor.transpose(banks[2 + b // 2][:, (b % 2) * D + k * P:(b % 2) * D + (k + 1) * P],
                                                w_exp[:, b, k * P:(k + 1) * P], ident[:, :])
                    if b % 2:
                        t.then_inc(upT_ps, 1)

            def fold_up(first):
                for b in range(first, first + 4):
                    nc.tensor.matmul(banks[2 + b % 4][:, 0:DA], bf_m[:, 0, b * P:(b + 1) * P], w_exp[:, b, :],
                                     start=True, stop=True).then_inc(up_ps, 1)

            def rows_T(s, h):
                pe.wait_ge(f_rows_loaded[s], 16 * (h + 1))
                for k in range(K):
                    for i in range(TT):
                        t = nc.tensor.transpose(banks[k][:, i * P:(i + 1) * P],
                                                f_rows[:, s, i, k * P:(k + 1) * P], ident[:, :])
                    t.then_inc(fT_ps, 1)

            def last_layer():
                pe.sem_inc(fy_free, 2)
                def products(p, s, h, last):
                    pe.wait_ge(fT_sb, K * (p + 1))
                    pe.sem_inc(f_rows_free, 1)
                    for f in range(FB):
                        if f >= 4 or not isinstance(p, int) or p > 0:
                            pe.wait_ge(fh_sb, FB * p + f - 3)
                        for k in range(K):
                            m = nc.tensor.matmul(banks[2 + f % 4][:, :], f_up[:, k, f * P:(f + 1) * P],
                                                 f_cols[:, k, :], start=(k == 0), stop=(k == K - 1))
                        m.then_inc(fh_ps, 1)
                    if not last:
                        rows_T(1 - s, h + s)
                    for i in range(TT):
                        if i == 0 and is_first(p):
                            pe.wait_ge(res_done, 4 * B)
                        if i % 2 == 0:
                            pe.wait_ge(fy_free, 2 * p + i // 2 + 1)
                        for f in range(FB):
                            if i == 0:
                                pe.wait_ge(fh_sb, FB * p + f + 1)
                            m = nc.tensor.matmul(banks[6 + i // 2][:, (i % 2) * D:(i % 2 + 1) * D],
                                                 f_hid[:, f, i * P:(i + 1) * P], f_down[:, f, :],
                                                 start=(f == 0), stop=(f == FB - 1))
                        if i % 2:
                            m.then_inc(fy_ps, 1)

                products(0, 0, 0, False)
                products(1, 1, 0, False)
                with pe.Fori(1, B // 2 - 1) as h:
                    for s in range(2):
                        products(2 * h + s, s, h, False)
                products(B - 2, 0, B // 2 - 1, False)
                products(B - 1, 1, B // 2 - 1, True)

            mamba(0)
            experts()
            mamba(1)
            last_layer()

        @block.vector
        def _(dve):
            def conv(p, g, h):
                ge(dve, xin_sb, C * g + 2 * h + 2)
                for k in range(PAD):
                    if k:
                        ge(dve, conv_tap, C * PAD * g + 2 * PAD * h + 2 * k)
                    for c in (2 * h, 2 * h + 1):
                        nc.vector.scalar_tensor_tensor(
                            out=chunk(u, p, c), in0=xpad[:, c, k:k + L], scalar=conv_w[:, c, k:k + 1],
                            in1=chunk(u, p, c), op0=ALU.mult, op1=ALU.add).then_inc(conv_tap, 1)

            def deltas(p, g):
                ge(dve, ln_ready, g + 1)
                d3 = half(delta, p).rearrange("p (c l) -> p c l", c=C)
                nc.vector.tensor_tensor(out=d3, in0=d3, in1=xpad[:, :, PAD:PAD + L],
                                        op=ALU.add).then_inc(delta_ready, 1)

            def scan(b, g, n):
                ge(dve, dA_ready, N * g + n + 1)
                ge(dve, dbu_made, N * g + n + 1)
                h = hst[:, n % HS, :, :].rearrange("p c l -> p (c l)")
                nc.vector.tensor_tensor_scan(out=h, data0=dA[:, n % AS, :, :].rearrange("p c l -> p (c l)"),
                                             data1=h, initial=0.0, op0=ALU.mult,
                                             op1=ALU.add).then_inc(scan_done, 1)

            def add_skip(e, g):
                ge(dve, y_summed, N * (g + 1))
                for c in range(C):
                    nc.vector.scalar_tensor_tensor(out=chunk(u, e, c), in0=chunk(u, e, c),
                                                   scalar=chan[:, 2, c:c + 1], in1=yb[c][:, :],
                                                   op0=ALU.mult, op1=ALU.add).then_inc(y_free, 1)

            def gate(e, g):
                ge(dve, y_free, C * (g + 1))
                ge(dve, zs_ready, g + 1)
                nc.vector.tensor_tensor(out=yz[:, :, :], in0=half(u, e).rearrange("p (c l) -> p c l", c=C),
                                        in1=yz[:, :, :], op=ALU.mult).then_inc(yz_ready, 1)

            def rows(e, i, n):
                return x[:, bass.ds(e * TT + i, n), :]

            def residual(e, g, j):
                ge(dve, out_ps, 2 * g + j + 1)
                r = rows(e, 2 * j, 2)
                nc.vector.tensor_tensor(out=r, in0=r, in1=pj[2 + j][:, :].rearrange("p (i d) -> p i d", d=D),
                                        op=ALU.add).then_inc(res_done, 1)

            def norm_stats(e, g):
                for i in range(TT):
                    s = nc.vector.bn_stats(out=stats[:, i, :], in_=rows(e, i, 1).rearrange("p o d -> p (o d)"))
                s.then_inc(stat_done, 1)
                ge_alone(dve, stat_done, g + 1)
                for i in range(TT):
                    s = nc.vector.bn_aggr(out=mv[:, i, :], in_=stats[:, i, :])
                s.then_inc(aggr_done, 1)
                ge_alone(dve, aggr_done, g + 1)
                nc.vector.tensor_scalar(ve[:, :], mv[:, :, 1], EPS, None, ALU.add).then_inc(var_ready, 1)

            def norm_apply(e, g):
                ge(dve, rstd_ready, g + 1)
                for i in range(TT):
                    r = rows(e, i, 1).rearrange("p o d -> p (o d)")
                    s = nc.vector.tensor_scalar(r, r, mv[:, i, 0:1], rstd[:, i:i + 1], ALU.subtract, ALU.mult)
                s.then_inc(norm_done, 1)

            def mamba(lay):
                def before():
                    g = lay * B
                    if lay == 0:
                        dve.sem_inc(shift_free, 1)
                    if lay:
                        dve.wait_ge(dense_stored, 32)
                    nc.vector.memset(xpad[:, :, 0:PAD], 0.0)
                    nc.vector.memset(dA[:, :, :, 0:1], 0.0).then_inc(pads_zeroed, 1)
                    dve.wait_ge(pads_zeroed, lay + 1)
                    dve.wait_ge(w_loaded, 16 * W_DMAS * (lay + 1))
                    dve.wait_ge(a_exp, lay + 1)
                    nc.vector.tensor_scalar(a_neg[:, :, :], a_neg[:, :, :], -1.0, None, ALU.mult).then_inc(a_ready, 1)
                    if lay:
                        norm_experts(0, 1)
                    conv(0, g, 0)
                    conv(0, g, 1)
                    if lay:
                        norm_experts(1, B // 2 - 1)
                    deltas(0, g)
                    if lay:
                        norm_expert(B - 1, 0, 0)

                def body(b):
                    g = b + lay * B
                    scan(b, g, 0)
                    for n in range(N):
                        if 0 < n < N - 1:
                            scan(b, g, n + 1)
                        ge(dve, scan_done, N * g + n + 1)
                        ge(dve, c_loaded[n % BCS], 16 * (N // BCS * g + n // BCS + 1))
                        ge(dve, y_summed, N * g + n - 1)
                        nc.vector.tensor_tensor(out=prod[:, n % 2, :, :], in0=hst[:, n % HS, :, :],
                                                in1=c_row[:, n % BCS:n % BCS + 1, :].broadcast_to([P, C, L]),
                                                op=ALU.mult).then_inc(prod_made, 1)
                        if n == 0:
                            if not is_first(b):
                                add_skip(b - 1, g - 1)
                            scan(b, g, 1)
                        if not is_first(b) and n == DVE_AT["gate"]:
                            gate(b - 1, g - 1)
                        if not is_last(b):
                            for h in range(2):
                                if n == DVE_AT["conv"][h]:
                                    conv(b + 1, g + 1, h)
                        if not is_first(b):
                            for h in range(2):
                                if n == DVE_AT["res"][h]:
                                    residual(b - 1, g - 1, h)
                            if n == DVE_AT["stats"]:
                                ge_alone(dve, res_done, 2 * g)
                                ge_alone(dve, shift_free, b + lay * (B - 1))
                                norm_stats(b - 1, g - 1 + lay * B)
                            if n == DVE_AT["shift"]:
                                ge(dve, rstd_ready, g + lay * B)
                                nc.vector.scalar_tensor_tensor(
                                    out=shift[:, :], in0=mv[:, :, 0], scalar=-1.0, in1=rstd[:, :],
                                    op0=ALU.mult, op1=ALU.mult).then_inc(shift_made, 1)

                over_batches(dve, before, body)
                e, g = B - 1, lay * B + B - 1
                add_skip(e, g)
                gate(e, g)
                residual(e, g, 0)
                residual(e, g, 1)
                dve.wait_ge(res_done, 2 * g + 2)
                dve.wait_ge(shift_free, (lay + 1) * (B - 1) + 1)
                norm_stats(e, g + lay * B)
                norm_apply(e, g + lay * B)

            def experts():
                step = [0]

                def link(i):
                    step[0] += 1
                    i.then_inc(route, 1)
                    dve.wait_ge(route, step[0])

                V = nc.vector
                dve.sem_inc(yt_made, 2)
                dve.wait_ge(g_cols_free, B + 2)
                dve.wait_ge(moe_const, 8)
                te = [P, NT, E]
                link(V.tensor_tensor(out=lg[:, :, :], in0=pj[0][:, 0:NT * E].rearrange("p (t e) -> p t e", e=E),
                                     in1=gate_b[:, :, :].broadcast_to(te), op=ALU.add))
                link(V.tensor_reduce(out=top[:, :], in_=lg[:, :, :], axis=AX.X, op=ALU.max))
                topb = top[:, :].rearrange("p (t o) -> p t o", o=1).broadcast_to(te)
                link(V.tensor_tensor(out=eq[:, :, :], in0=lg[:, :, :], in1=topb, op=ALU.subtract))
                link(V.tensor_tensor(out=lg[:, :, :], in0=lg[:, :, :], in1=topb, op=ALU.is_equal))
                link(V.tensor_tensor(out=lg[:, :, :], in0=lg[:, :, :], in1=prio[:, :, :].broadcast_to(te),
                                     op=ALU.mult))
                link(V.tensor_reduce(out=top[:, :], in_=lg[:, :, :], axis=AX.X, op=ALU.max))
                V.tensor_tensor(out=pick[:, :, :], in0=lg[:, :, :], in1=topb, op=ALU.is_equal).then_inc(picked, 1)
                dve.wait_ge(gate_exp, 1)
                link(V.tensor_reduce(out=w_top[:, :], in_=eq[:, :, :], axis=AX.X, op=ALU.add))
                link(V.reciprocal(w_top[:, :], w_top[:, :]))
                dve.wait_ge(ranked, 1)
                et = [P, E, NT]
                link(V.tensor_copy(tot[:, :, :], pj[2][:, 0:NT * E].rearrange("p (t e) -> p e t", e=E)))
                link(V.tensor_tensor_scan(out=cum[:, :, :].rearrange("p e t -> p (e t)"),
                                          data0=restart[:, :, :].rearrange("p e t -> p (e t)"),
                                          data1=tot[:, :, :].rearrange("p e t -> p (e t)"),
                                          initial=0.0, op0=ALU.mult, op1=ALU.add))
                es = [P, E, SMAX]
                link(V.tensor_tensor(out=cmp_s[:, :, :], in0=cum[:, :, NT - 1:NT].broadcast_to(es),
                                     in1=steps[:, :, :].broadcast_to(es), op=ALU.is_gt))
                link(V.tensor_reduce(out=n_tiles[:, :], in_=cmp_s[:, :, :], axis=AX.X, op=ALU.add))
                link(V.tensor_tensor_scan(out=end_tile[:, :], data0=ones[:, 0:E], data1=n_tiles[:, :],
                                          initial=0.0, op0=ALU.mult, op1=ALU.add))
                link(V.tensor_tensor(out=first_tile[:, :], in0=end_tile[:, :], in1=n_tiles[:, :], op=ALU.subtract))
                link(V.tensor_tensor(out=cum[:, :, :], in0=cum[:, :, :], in1=tot[:, :, :], op=ALU.subtract))
                link(V.scalar_tensor_tensor(
                    out=cum[:, :, :], in0=first_tile[:, :].rearrange("p (e o) -> p e o", o=1).broadcast_to(et),
                    scalar=float(TS), in1=cum[:, :, :], op0=ALU.mult, op1=ALU.add))
                link(V.tensor_tensor(out=lg[:, :, :], in0=cum[:, :, :].rearrange("p e t -> p t e"),
                                     in1=pj[1][:, 0:NT * E].rearrange("p (t e) -> p t e", e=E), op=ALU.add))
                link(V.tensor_tensor(out=lg[:, :, :], in0=lg[:, :, :], in1=pick[:, :, :], op=ALU.mult))
                link(V.tensor_reduce(out=dest_f[:, :], in_=lg[:, :, :], axis=AX.X, op=ALU.add))
                link(V.tensor_copy(dest[:, :], dest_f[:, :]))
                ct = [P, TILES, E]
                link(V.tensor_tensor(out=cmp_t[:, :, :],
                                     in0=end_tile[:, :].rearrange("p (o e) -> p o e", o=1).broadcast_to(ct),
                                     in1=tile_no[:, :, :].broadcast_to(ct), op=ALU.is_le))
                link(V.tensor_reduce(out=tile_e[:, :], in_=cmp_t[:, :, :], axis=AX.X, op=ALU.add))
                link(V.tensor_scalar(tile_e[:, :], tile_e[:, :], float(E - 1), None, ALU.min))
                link(V.tensor_copy(tile_i[:, :], tile_e[:, :]))
                dve.sem_inc(routed, 1)

                dve.wait_ge(far_loaded, 64)
                far_stages(va, vb, va, 1, D)

                def tile(j, s, h):
                    dve.wait_ge(yt_ps, j + 1)
                    if not isinstance(h, int) or h > 0:
                        ge_alone(dve, y_stored[s], 16 * h)
                    V.tensor_tensor(out=yt[:, s, :, :],
                                    in0=banks[6 + s][:, :].rearrange("p (r d) -> p r d", d=D),
                                    in1=b2[:, s:s + 1, :].broadcast_to([P, TR, D]), op=ALU.add).then_inc(yt_made, 1)

                tile(0, 0, 0)
                tile(1, 1, 0)
                with dve.Fori(1, (TILES - FOLDS) // 2) as h:
                    for s in range(2):
                        tile(2 * h + s, s, h)
                for j in range(TILES - FOLDS, TILES - 2):
                    tile(j, j % 2, j // 2)
                dve.wait_ge(up_sb, FB)
                far_stages(va, w_exp, va, 0, DA)
                V.tensor_tensor(out=gelu_b[:, :], in0=w_exp[:, :, D], in1=up_b[:, :], op=ALU.add)
                for j in range(TILES - 2, TILES):
                    tile(j, j % 2, j // 2)
                add_expert(0, 0, 0)
                norm_expert(0, 1, 0)

            def add_expert(e, s, h):
                for i in range(TT):
                    t = e * TT + i
                    if i == 0:
                        ge_alone(dve, gathered[s], 16 * TT * (h + 1))
                    r = rows(e, i, 1).rearrange("p o d -> p (o d)")
                    a = nc.vector.scalar_tensor_tensor(
                        out=r, in0=yg[:, s, i, :], scalar=w_top[:, bass.ds(t, 1)], in1=r, op0=ALU.mult, op1=ALU.add)
                a.then_inc(gathered_added, 1)

            def norm_expert(e, s, h):
                ge_alone(dve, gathered_added, e + 1)
                norm_stats(e, B + e)
                if not is_last(e):
                    add_expert(e + 1, s, h)
                norm_apply(e, B + e)

            def norm_experts(lo, hi):
                with dve.Fori(lo, hi) as h:
                    norm_expert(2 * h + 1, 0, h + 1)
                    norm_expert(2 * h + 2, 1, h + 1)

            def far_stages(src, dst, mid, half_, width):
                order = range(FAR) if half_ == 0 else range(FAR - 1, -1, -1)
                bufs = [src, dst, mid, dst]
                for n, stage in enumerate(order):
                    bl = 1 << stage
                    a_in = bufs[n][:, :, 0:width].rearrange("p (n two b) d -> p n two b d", two=2, b=bl)
                    a_out = bufs[n + 1][:, :, 0:width].rearrange("p (n two b) d -> p n two b d", two=2, b=bl)
                    w = far_w[:, half_, stage, :, :].rearrange("p (n b) w -> p n b w", b=bl)
                    shape = [P, FB // 2 // bl, bl, width]
                    tmp = [far_t[:, t, :, 0:width].rearrange("p (n b) d -> p n b d", b=bl) for t in range(2)]
                    for r in range(2):
                        for c in range(2):
                            wi = 2 * r + c if half_ == 0 else 2 * c + r
                            i = nc.vector.tensor_tensor(out=tmp[c], in0=a_in[:, :, c, :, :],
                                                        in1=w[:, :, :, wi:wi + 1].broadcast_to(shape), op=ALU.mult)
                        i.then_inc(far_part, 1)
                        far_parts[0] += 1
                        dve.wait_ge(far_part, far_parts[0])
                        i = nc.vector.tensor_tensor(out=a_out[:, :, r, :, :], in0=tmp[0], in1=tmp[1], op=ALU.add)
                        i.then_inc(far_part, 1)
                        far_parts[0] += 1
                        dve.wait_ge(far_part, far_parts[0])
                dve.sem_inc(far_step, 9)

            far_parts = [0]

            def last_layer():
                with dve.Fori(0, B) as p:
                    for j in range(2):
                        dve.wait_ge(fy_ps, 2 * p + j + 1)
                        r = rows(p, 2 * j, 2)
                        nc.vector.tensor_tensor(out=r, in0=r,
                                                in1=banks[6 + j][:, :].rearrange("p (i d) -> p i d", d=D),
                                                op=ALU.add).then_inc(fy_free, 1)
                    dve.wait_ge(fy_free, 2 * p + 4)
                    r = rows(p, 0, TT)
                    for half_ in range(2):
                        nc.vector.tensor_tensor(out=r, in0=r,
                                                in1=f_bias[:, half_:half_ + 1, :].broadcast_to([P, TT, D]),
                                                op=ALU.add).then_inc(f_added, 1)
                        ge_alone(dve, f_added, 2 * p + half_ + 1)
                    norm_stats(p, 3 * B + p)
                    norm_apply(p, 3 * B + p)

            mamba(0)
            experts()
            mamba(1)
            last_layer()


def kernel(**inputs):
    import numpy as np
    import concourse.bacc as bacc
    from concourse import mybir as mb
    from concourse.bass_utils import run_bass_kernel_spmd

    nc = bacc.Bacc("TRN2", target_bir_lowering=False, num_devices=1, dynamic_dma_scratch_size=4096)
    A = {k: np.asarray(v) for k, v in inputs.items()}

    def per_channel(v):
        return v.reshape(-1, 128).T

    def state_rows_in_pairs(w, rank):
        n = (w.shape[0] - rank) // 2
        b, c = w[rank:rank + n], w[rank + n:]
        return np.concatenate([np.stack([b, c], 1).reshape(2 * n, -1), w[:rank]], 0).T

    lay = {"L0_x": A["L0_attn_hidden_states"]}
    names = {0: ("conv1d_w", "conv1d_b", "D_param"), 1: ("conv_w", "conv_b", "D")}
    for n in (0, 1):
        q, (cw, cb, dn) = f"L{n}_attn_", names[n]
        lay[f"L{n}_w_in"] = A[q + "in_proj_w"].T
        lay[f"L{n}_conv_w"] = A[q + cw].reshape(-1, A[q + cw].shape[-1])
        lay[f"L{n}_conv_b"] = per_channel(A[q + cb])
        lay[f"L{n}_w_x"] = state_rows_in_pairs(A[q + "x_proj_w"], A[q + "dt_proj_w"].shape[1])
        lay[f"L{n}_dt_w"] = A[q + "dt_proj_w"].T
        lay[f"L{n}_dt_b"] = per_channel(A[q + "dt_proj_b"])
        lay[f"L{n}_A_log"] = A[q + "A_log"]
        lay[f"L{n}_D"] = per_channel(A[q + dn])
        lay[f"L{n}_w_out"] = A[q + "out_proj_w"].T
    f0, f1 = "L0_ffn_", "L1_ffn_"
    lay["gate_w"], lay["gate_b"] = A[f0 + "Wg"], A[f0 + "bg"].reshape(1, -1)
    lay["W1"], lay["W2"], lay["b2"] = A[f0 + "W1"], A[f0 + "W2"], A[f0 + "b2"]
    lay["b1"] = A[f0 + "b1"].reshape(A[f0 + "b1"].shape[0], -1, 128).transpose(0, 2, 1)
    lay["w_exp"] = np.concatenate([A[f1 + "W_exp"], A[f1 + "b_exp"].reshape(1, -1)], 0).T
    lay["w_con"] = A[f1 + "W_con"]
    for k, name in (("up_w", "up_weights"), ("down_w", "down_weights")):
        lay[k] = A[f1 + name].reshape(*A[f1 + name].shape[:2], 4)
    lay["up_bias"] = per_channel(A[f1 + "up_bias"])
    lay["b_con"], lay["down_bias"] = A[f1 + "b_con"].reshape(1, -1), A[f1 + "down_bias"].reshape(1, -1)
    arrays, hbm = {}, {}
    for k, v in lay.items():
        arrays["in_" + k] = a = np.ascontiguousarray(v)
        hbm[k] = nc.dram_tensor("in_" + k, a.shape, mb.dt.from_np(a.dtype), kind="ExternalInput").ap()
    shape = A["L0_attn_hidden_states"].shape
    out = nc.dram_tensor("out", shape, mb.dt.float32, kind="ExternalOutput").ap()
    build(nc, hbm, out)
    got = run_bass_kernel_spmd(nc, [arrays], core_ids=[0])
    return got.results[0]["out"]
```
